# Optimizing a Trainium2 kernel written in Bass

```python
import numpy as np
import jax
import jax.numpy as jnp

def _softmax(x, axis=-1):
    return jax.nn.softmax(x, axis=axis)

def _gelu(x):
    return jax.nn.gelu(x, approximate=True)

def _silu(x):
    return jax.nn.silu(x)

def _sigmoid(x):
    return jax.nn.sigmoid(x)

def _layernorm(x, axis=-1, eps=1e-05):
    m = jnp.mean(x, axis=axis, keepdims=True)
    v = jnp.var(x, axis=axis, keepdims=True)
    return (x - m) / jnp.sqrt(v + eps)

def _scatter_add(tgt, idx, src, axis=0):
    return tgt.at[idx].add(src)

def _segment_sum(src, seg, n):
    return jax.ops.segment_sum(src, seg, n)
kernel_name = 'mk_hybrid_d1_jaxref_r4_8af4b9'

def setup_inputs(seed: int=0):
    np.random.seed(seed)
    _w = jnp.asarray

    def _L0_attn_a_setup():
        import jax, jax.numpy as jnp
        import numpy as np
        B, N, D, H = (4, 1024, 256, 16)
        HD = D // H

        def _kernel(x):
            return jax.nn.elu(x) + 1.0
        key = jax.random.key(seed)
        k1, k2, k3, k4 = jax.random.split(key, 4)
        x = jax.random.normal(k1, (B, N, D), dtype=jnp.float32)
        w_qkv = jax.random.normal(k2, (3 * D, D), dtype=jnp.float32) * (1.0 / np.sqrt(D))
        w_out = jax.random.normal(k3, (D, D), dtype=jnp.float32) * (1.0 / np.sqrt(D))
        b_out = jax.random.normal(k4, (D,), dtype=jnp.float32) * 0.01
        return {'x': x, 'w_qkv': w_qkv, 'w_out': w_out, 'b_out': b_out}
    _L0_attn_a_in = _L0_attn_a_setup()

    def _L0_attn_b_setup():
        import jax, jax.numpy as jnp
        import numpy as np
        EPS = 1e-05

        def _proj_ln(x, W, b, g, beta):
            y = jnp.einsum('blc,cd->bld', x, W) + b
            mu = jnp.mean(y, axis=-1, keepdims=True)
            var = jnp.var(y, axis=-1, keepdims=True)
            return (y - mu) * jax.lax.rsqrt(var + EPS) * g + beta
        key = jax.random.key(seed)
        B, L, C, H = (4, 512, 256, 256)
        ks = jax.random.split(key, 7)
        s_in = 1.0 / np.sqrt(C)
        inp = {'input_sequence': jax.random.normal(ks[0], (B, L, C), jnp.float32), 'Wk': jax.random.normal(ks[1], (C, H), jnp.float32) * s_in, 'bk': jnp.zeros((H,), jnp.float32), 'gk': jnp.ones((H,), jnp.float32), 'betak': jnp.zeros((H,), jnp.float32), 'Wq': jax.random.normal(ks[2], (C, H), jnp.float32) * s_in, 'bq': jnp.zeros((H,), jnp.float32), 'gq': jnp.ones((H,), jnp.float32), 'betaq': jnp.zeros((H,), jnp.float32), 'Wv': jax.random.normal(ks[3], (C, C), jnp.float32) * s_in, 'bv': jnp.zeros((C,), jnp.float32), 'gv': jnp.ones((C,), jnp.float32), 'betav': jnp.zeros((C,), jnp.float32)}
        return inp
    _L0_attn_b_in = _L0_attn_b_setup()

    def _L0_ffn_setup():
        import jax, jax.numpy as jnp
        import numpy as np
        NUM_EXPERTS = 8
        TOP_K = 2
        key = jax.random.key(seed)
        ks = jax.random.split(key, 4)
        B, S, H, F = (4, 1024, 256, 1024)
        x = jax.random.normal(ks[0], (B, S, H), dtype=jnp.float32)
        router_w = jax.random.normal(ks[1], (H, NUM_EXPERTS), dtype=jnp.float32) * 0.02
        w1 = jax.random.normal(ks[2], (H, F), dtype=jnp.float32) * 0.02
        b1 = jnp.zeros((F,), dtype=jnp.float32)
        w2 = jax.random.normal(ks[3], (F, H), dtype=jnp.float32) * 0.02
        b2 = jnp.zeros((H,), dtype=jnp.float32)
        return {'x': x, 'router_w': router_w, 'w1': w1, 'b1': b1, 'w2': w2, 'b2': b2}
    _L0_ffn_in = _L0_ffn_setup()
    _d = {'L0_attn_a_x': _L0_attn_a_in['x'], 'L0_attn_a_w_qkv': _L0_attn_a_in['w_qkv'], 'L0_attn_a_w_out': _L0_attn_a_in['w_out'], 'L0_attn_a_b_out': _L0_attn_a_in['b_out'], 'L0_attn_b_Wk': _L0_attn_b_in['Wk'], 'L0_attn_b_bk': _L0_attn_b_in['bk'], 'L0_attn_b_gk': _L0_attn_b_in['gk'], 'L0_attn_b_betak': _L0_attn_b_in['betak'], 'L0_attn_b_Wq': _L0_attn_b_in['Wq'], 'L0_attn_b_bq': _L0_attn_b_in['bq'], 'L0_attn_b_gq': _L0_attn_b_in['gq'], 'L0_attn_b_betaq': _L0_attn_b_in['betaq'], 'L0_attn_b_Wv': _L0_attn_b_in['Wv'], 'L0_attn_b_bv': _L0_attn_b_in['bv'], 'L0_attn_b_gv': _L0_attn_b_in['gv'], 'L0_attn_b_betav': _L0_attn_b_in['betav'], 'L0_ffn_router_w': _L0_ffn_in['router_w'], 'L0_ffn_w1': _L0_ffn_in['w1'], 'L0_ffn_b1': _L0_ffn_in['b1'], 'L0_ffn_w2': _L0_ffn_in['w2'], 'L0_ffn_b2': _L0_ffn_in['b2']}
    _x0 = _d['L0_attn_a_x']
    _d['L0_attn_a_x'] = jax.random.normal(jax.random.fold_in(jax.random.key(seed), 1), (16, 512, 256), dtype=_x0.dtype)
    del _x0
    return _d

def reference(L0_attn_a_x, L0_attn_a_w_qkv, L0_attn_a_w_out, L0_attn_a_b_out, L0_attn_b_Wk, L0_attn_b_bk, L0_attn_b_gk, L0_attn_b_betak, L0_attn_b_Wq, L0_attn_b_bq, L0_attn_b_gq, L0_attn_b_betaq, L0_attn_b_Wv, L0_attn_b_bv, L0_attn_b_gv, L0_attn_b_betav, L0_ffn_router_w, L0_ffn_w1, L0_ffn_b1, L0_ffn_w2, L0_ffn_b2):

    def _L0_attn_a_ref(x, w_qkv, w_out, b_out):
        import jax, jax.numpy as jnp
        import numpy as np
        B, N, D, H = (4, 1024, 256, 16)
        HD = D // H

        def _kernel(x):
            return jax.nn.elu(x) + 1.0
        b, n, d = x.shape
        qkv = x @ w_qkv.T
        qkv = qkv.reshape(b, n, 3, H, HD)
        q, k, v = (qkv[:, :, 0], qkv[:, :, 1], qkv[:, :, 2])
        q = _kernel(q)
        k = _kernel(k)
        kv = jnp.einsum('bnhd,bnhm->bhdm', k, v)
        z = 1.0 / (jnp.einsum('bnhd,bhd->bnh', q, k.sum(axis=1)) + 1e-06)
        out = jnp.einsum('bnhd,bhdm,bnh->bnhm', q, kv, z)
        out = out.reshape(b, n, d)
        return out @ w_out.T + b_out

    def _L0_attn_b_ref(input_sequence, Wk, bk, gk, betak, Wq, bq, gq, betaq, Wv, bv, gv, betav):
        import jax, jax.numpy as jnp
        import numpy as np
        EPS = 1e-05

        def _proj_ln(x, W, b, g, beta):
            y = jnp.einsum('blc,cd->bld', x, W) + b
            mu = jnp.mean(y, axis=-1, keepdims=True)
            var = jnp.var(y, axis=-1, keepdims=True)
            return (y - mu) * jax.lax.rsqrt(var + EPS) * g + beta
        values = _proj_ln(input_sequence, Wv, bv, gv, betav)
        k = _proj_ln(input_sequence, Wk, bk, gk, betak)
        q = _proj_ln(input_sequence, Wq, bq, gq, betaq)
        scores = jnp.einsum('blc,bLc->blL', k, q)
        attn = jax.nn.softmax(scores, axis=-1)
        out = jnp.einsum('blL,bLc->blc', attn, values)
        return out + input_sequence

    def _L0_ffn_ref(x, router_w, w1, b1, w2, b2):
        import jax, jax.numpy as jnp
        import numpy as np
        NUM_EXPERTS = 8
        TOP_K = 2
        B, S, H = x.shape
        xt = x.reshape(-1, H)
        router_logits = jnp.matmul(xt, router_w)
        router_probs = jax.nn.softmax(router_logits, axis=-1)
        top_k_probs, top_k_indices = jax.lax.top_k(router_probs, TOP_K)
        top_k_probs = top_k_probs / jnp.sum(top_k_probs, axis=-1, keepdims=True)
        one_hot = jax.nn.one_hot(top_k_indices, NUM_EXPERTS, dtype=xt.dtype)
        combine = jnp.einsum('tk,tke->te', top_k_probs, one_hot)
        expert_out = jnp.matmul(jax.nn.gelu(jnp.matmul(xt, w1) + b1), w2) + b2
        out = expert_out * jnp.sum(combine, axis=-1, keepdims=True)
        return out.reshape(B, S, H)
    x = L0_attn_a_x
    x = x + _L0_attn_a_ref(_layernorm(x, axis=-1), L0_attn_a_w_qkv, L0_attn_a_w_out, L0_attn_a_b_out)
    x = x + _L0_ffn_ref(_layernorm(x, axis=-1), L0_ffn_router_w, L0_ffn_w1, L0_ffn_b1, L0_ffn_w2, L0_ffn_b2)
    x = x + _L0_attn_b_ref(_layernorm(x, axis=-1), L0_attn_b_Wk, L0_attn_b_bk, L0_attn_b_gk, L0_attn_b_betak, L0_attn_b_Wq, L0_attn_b_bq, L0_attn_b_gq, L0_attn_b_betaq, L0_attn_b_Wv, L0_attn_b_bv, L0_attn_b_gv, L0_attn_b_betav)
    x = x + _L0_ffn_ref(_layernorm(x, axis=-1), L0_ffn_router_w, L0_ffn_w1, L0_ffn_b1, L0_ffn_w2, L0_ffn_b2)
    return x

_drawn_inputs = setup_inputs


def setup_inputs(seed=0):
    import zlib

    import numpy as np

    out = dict(_drawn_inputs(seed))
    spreads = {'L0_attn_b_bk': (0.0, 0.1),
     'L0_attn_b_gk': (1.0, 0.2),
     'L0_attn_b_betak': (0.0, 0.1),
     'L0_attn_b_bq': (0.0, 0.1),
     'L0_attn_b_gq': (1.0, 0.2),
     'L0_attn_b_betaq': (0.0, 0.8),
     'L0_attn_b_bv': (0.0, 0.1),
     'L0_attn_b_gv': (1.0, 0.2),
     'L0_attn_b_betav': (0.0, 0.1),
     'L0_ffn_b1': (0.0, 0.1),
     'L0_ffn_b2': (0.0, 0.1)}
    factors = {'L0_attn_a_b_out': 3.395, 'L0_ffn_router_w': 8.0}
    for name, (base, spread) in spreads.items():
        noise = np.random.default_rng([zlib.crc32(name.encode()), seed]).standard_normal(out[name].shape)
        drawn = base * np.exp(spread * noise) if base else spread * noise
        out[name] = jnp.asarray(drawn.astype(out[name].dtype))
    for name, factor in factors.items():
        out[name] = (out[name] * factor).astype(out[name].dtype)
    return out
```

```python
from contextlib import ExitStack

import concourse.bass as bass
from concourse import mybir

F32 = mybir.dt.float32
F32R = mybir.dt.float32r
BF16 = mybir.dt.bfloat16
ALU = mybir.AluOpType
ACT = mybir.ActivationFunctionType
X_AXIS = mybir.AxisListType.X

P = 128
PARTS = ("hi", "lo")


class Turn:

    def __init__(self, multiples, scale, offset):
        self.multiples, self.scale, self.offset = multiples, scale, offset

    def __add__(self, n):
        return Turn(self.multiples, self.scale, self.offset + n)

    def __sub__(self, n):
        return self + -n

    def times(self, n):
        return Turn(self.multiples, self.scale * n, self.offset * n)


def turns(eng, i):
    multiples = {m: eng.snap(i * m) for m in (1, 2, 4, 8, 16)}
    batch = Turn(multiples, 1, 0)
    return batch, batch.times(2) - 1


def at(turn, per_turn, k):
    if isinstance(turn, Turn):
        count = turn.offset * per_turn + k
        value = turn.multiples[turn.scale * per_turn]
        return value + count if count else value
    return turn * per_turn + k


def hybrid_block(nc, x, w_qkv, w_out, b_out, w_kqv, b_kqv, kq_gain, v_gain, v_beta,
                 router_w, w1, b1, w2, b2, out):
    NB, N, D = x.shape
    T = N // P
    C = D // P
    FF = w1.shape[1]
    NF = FF // P
    E = router_w.shape[1]
    HD = 16
    EPS = 1e-5
    assert (T, C, N, E) == (4, 2, 512, 8) and NF == 8

    with ExitStack() as ctx:
        def sb(name, shape, dt=F32, cx=ctx):
            return cx.enter_context(nc.sbuf_tensor(name, shape, dt))

        def split(name, shape):
            return [sb(f"{name}_{part}", shape, F32R) for part in PARTS]

        def sem(name):
            return ctx.enter_context(nc.semaphore(name))

        wqkv_s = split("wqkv", [P, C, 3 * D])
        wout_s = split("wout", [P, C, D])
        wkqv_s = split("wkqv", [P, C, 3 * D])
        wr_s = split("wr", [P, C, E])
        w1_s = split("w1", [P, C, FF])
        w2_s = split("w2", [P, NF, D])
        ident = sb("ident", [P, P])
        head_mask = sb("head_mask", [P, P])
        ones_r = sb("ones_r", [P, 2], F32R)
        ones_b = sb("ones_b", [P, P], BF16)
        bout_rows = sb("bout_rows", [P, 2, D], BF16)
        b2_rows = sb("b2_rows", [P, 2, D], BF16)
        bkqv_rows = sb("bkqv_rows", [P, 3 * D], BF16)
        kq_gain_sb = sb("kq_gain_sb", [P, 4 * C])
        b1_sb = sb("b1_sb", [P, NF])
        v_gain_sb = sb("v_gain_sb", [P, D])
        v_beta_sb = sb("v_beta_sb", [P, D])
        neg_half = sb("neg_half", [P, 3 * T])
        z_eps = sb("z_eps", [P, 1])
        SPARE = 256
        spare_dve, spare_pool = sb("spare_dve", [P, SPARE], BF16), sb("spare_pool", [P, SPARE], BF16)
        stA, stF, stK = sb("stA", [P, T, 6]), sb("stF", [P, T, 6]), sb("stK", [P, T, 3, 6])
        mvA, mvF, mvK = sb("mvA", [P, T, 2]), sb("mvF", [P, T, 2]), sb("mvK", [P, T, 3, 2])
        rsA, rsF, rsK = sb("rsA", [P, T]), sb("rsF", [P, T]), sb("rsK", [P, T, 3])
        veA, veF, veK = sb("veA", [P, T]), sb("veF", [P, T]), sb("veK", [P, T, 3])
        top = sb("top", [P, T, E])
        top_p = sb("top_p", [P, T, E])
        p_sum, p_rec = sb("p_sum", [P, T]), sb("p_rec", [P, T])
        t_sum, t_rec = sb("t_sum", [P, T]), sb("t_rec", [P, T])
        comb = sb("comb", [P, T])
        p2 = sb("p2", [P, T, 2])
        row_negmax, row_sum, row_rec = sb("row_negmax", [P, T]), sb("row_sum", [P, T]), sb("row_rec", [P, T])
        x_in = sb("x_in", [P, T, D])
        xn_a = sb("xn_a", [P, T, D])
        xn_b = sb("xn_b", [P, T, D])
        xT_s = split("xT", [P, C, N])
        q_f = sb("q_f", [P, C, N])
        tmp = sb("tmp", [P, C, N])
        qT_s = split("qT", [P, C, N])
        k_s = split("k", [P, T, D])
        v_s = split("v", [P, T, D])
        v_f = sb("v_f", [P, T, D])
        km_f = sb("km_f", [P, 2 * C, P])
        km_s = split("km", [P, 2 * C, P])
        kvw_s = split("kvw", [P, C, D])
        stage_cx = ExitStack()
        NW = C * 3 * D * 2 + C * D + C * E + C * FF + NF * D
        stage = sb("stage", [P, NW], F32, stage_cx)
        bias_f = sb("bias_f", [1, 5 * D], F32, stage_cx)
        bias_b = sb("bias_b", [1, 3, 5 * D], BF16, stage_cx)
        stage_cx.close()
        x1 = sb("x1", [P, T, D])
        x1T_s = split("x1T", [P, C, N])
        x2 = sb("x2", [P, T, D])
        kq_n = sb("kq_n", [P, T, 2 * D])
        k_f = kq_n[:, :, 0:D]
        kqT_s = split("kqT", [P, 2 * C, N])
        x3 = sb("x3", [P, T, D])
        x3T_s = split("x3T", [P, C, N])
        HR = 4
        h_f = [sb(f"h_f{n}", [P, N]) for n in range(2)]
        h_s = [split(f"h{n}", [P, N]) for n in range(HR)]

        X = ctx.enter_context(nc.psum_tensor("X", [P, 2, 512], F32))
        Y = ctx.enter_context(nc.psum_tensor("Y", [P, 2, 512], F32))
        O = ctx.enter_context(nc.psum_tensor("O", [P, 2, 512], F32))
        H = [ctx.enter_context(nc.psum_tensor(f"H{n}", [P, 512], F32)) for n in range(2)]

        names = """w_in small_in bias_in bias_rows w_hi w_lo consts pool_const zeroed bias_part
        x_in x_out
        a_stats a_mv a_ve a_rstd a_xn a_xnT a_xT_hi a_xT_lo
        a_q a_q_exp a_q_relu a_q_f a_q_hi a_q_lo
        a_kv a_kv_exp a_kv_relu a_k_f a_k_hi a_k_lo a_v_hi a_v_lo
        a_km a_km_f a_km_hi a_km_lo a_kvw a_kvw_hi a_kvw_lo a_den a_den_eps a_z a_qz a_qz_hi a_qz_lo
        a_out a_x1 a1_stats a1_mv a1_ve a1_rstd a1_xn a1_xnT a1_xT_hi a1_xT_lo
        f_router f_top f_shift f_exp f_psum f_prec f_p2 f_tsum f_trec f_comb_p f_comb
        f_h f_gelu f_h_hi f_h_lo f_o f_y
        b_stats b_mv b_ve b_rstd b_xn b_res b_xnT b_xT_hi b_xT_lo
        b_kqv b_kqv_stats b_kqv_mv b_kqv_ve b_kqv_rstd b_kqv_n b_v_g b_v_f b_v_hi b_v_lo
        b_kT b_kT_f b_kT_hi b_kT_lo b_qT b_qT_f b_qT_hi b_qT_lo
        b_sc b_max b_prob b_pT b_pT_hi b_pT_lo b_rec b_out b_x3
        b3_stats b3_mv b3_ve b3_rstd b3_xn b3_xnT b3_xT_hi b3_xT_lo""".split()
        S = {n: sem(n) for n in names}

        places, base = [], 0
        for src, dst in ((w_qkv, wqkv_s), (w_out, wout_s), (router_w, wr_s), (w1, w1_s),
                         (w2, w2_s), (w_kqv, wkqv_s)):
            chunks, width = src.shape[0] // P, src.shape[1]
            view = stage[:, base:base + chunks * width].rearrange("p (c n) -> p c n", c=chunks)
            places.append((src, dst, view))
            base += chunks * width
        NWT = len(places)
        biases = ((b_out, 0, D), (b2, D, D), (b_kqv, 2 * D, 3 * D))

        block = ctx.enter_context(nc.Block())

        @block.sync
        def _(sp):
            def load_x(b, peeled=False):
                if not (peeled and b == 0):
                    sp.wait_ge(S["a_x1"], at(b, 1, 0))
                sp.dma_start(x_in[:], x[bass.ds(b, 1)].rearrange("o (t p) d -> p (o t) d", p=P)) \
                    .then_inc(S["x_in"], 16)

            def store_out(b):
                sp.wait_ge(S["f_y"], 2 * b + 3)
                sp.dma_start(out[bass.ds(b, 1)].rearrange("o (t p) d -> p (o t) d", p=P), x3[:]) \
                    .then_inc(S["x_out"], 16)

            for src, dst, view in places[:1]:
                sp.dma_start(view, src.rearrange("(c p) n -> p c n", p=P)).then_inc(S["w_in"], 16)
            load_x(0, True)
            for src, at0, width in biases:
                sp.dma_start(bias_f[0:1, at0:at0 + width], src).then_inc(S["bias_in"], 16)
            for src, dst, view in places[1:]:
                sp.dma_start(view, src.rearrange("(c p) n -> p c n", p=P)).then_inc(S["w_in"], 16)
            sp.dma_start(kq_gain_sb[:], kq_gain).then_inc(S["small_in"], 16)
            sp.dma_start(b1_sb[:], b1).then_inc(S["small_in"], 16)
            sp.dma_start(v_gain_sb[:], v_gain.partition_broadcast(P)).then_inc(S["small_in"], 16)
            sp.dma_start(v_beta_sb[:], v_beta.partition_broadcast(P)).then_inc(S["x_out"], 16)
            sp.wait_ge(S["bias_part"], 6)
            sp.wait_ge(S["zeroed"], 3)
            for row in range(3):
                for half in range(2):
                    sp.dma_start(bout_rows[row:row + 1, half, :], bias_b[0:1, row, 0:D]).then_inc(S["bias_rows"], 16)
                    sp.dma_start(b2_rows[row:row + 1, half, :], bias_b[0:1, row, D:2 * D]).then_inc(S["bias_rows"], 16)
                sp.dma_start(bkqv_rows[row:row + 1, :], bias_b[0:1, row, 2 * D:5 * D]).then_inc(S["bias_rows"], 16)
            load_x(1)
            load_x(2)
            with sp.Fori(1, NB - 2) as i:
                load_x(i + 2)
                store_out(i - 1)
            store_out(NB - 3)
            store_out(NB - 2)
            sp.wait_ge(S["f_y"], 2 * NB)
            sp.dma_start(out[NB - 1:NB].rearrange("o (t p) d -> p (o t) d", p=P), x3[:]).then_inc(S["x_out"], 16)
            sp.wait_ge(S["x_out"], 16 * (NB + 1))

        @block.tensor
        def _(pe):
            def mm3(dst, l_hi, l_lo, r_hi, r_lo, start, stop):
                pe.matmul(dst, l_hi, r_hi, start=start, stop=False, skip_group_check=True)
                pe.matmul(dst, l_hi, r_lo, start=False, stop=False, skip_group_check=True)
                return pe.matmul(dst, l_lo, r_hi, start=False, stop=stop, skip_group_check=True)

            def turn(dst, src, done):
                for c in range(C):
                    for t in range(T):
                        op = pe.transpose(dst[:, c, t * P:(t + 1) * P], src[:, t, c * P:(c + 1) * P], ident[:])
                op.then_inc(done, 1)

            def a_turn(b, prev):
                pe.wait_ge(S["a_xn"], at(b, 1, 1))
                if prev:
                    pe.wait_ge(S["b_pT_lo"], at(b - 1, 2, 0))
                elif b != 0:
                    pe.wait_ge(S["a1_xT_lo"], at(b, 1, 0))
                turn(X, xn_a, S["a_xnT"])

            def a_q(b, prev):
                pe.wait_ge(S["a_xT_hi"], at(b, 1, 1))
                pe.wait_ge(S["a_xT_lo"], at(b, 1, 1))
                if prev:
                    pe.wait_ge(S["b_x3"], at(b - 1, 1, 0))
                for m in range(C):
                    for k in range(C):
                        op = mm3(Y[:, m, :], wqkv_s[0][:, k, m * P:(m + 1) * P], wqkv_s[1][:, k, m * P:(m + 1) * P],
                                 xT_s[0][:, k, :], xT_s[1][:, k, :], k == 0, k == C - 1)
                op.then_inc(S["a_q"], 1)

            def a_kv(b, pair):
                dst = (X, Y)[pair]
                if pair:
                    pe.wait_ge(S["a_q_relu"], at(b, 1, 1))
                for t in range(2):
                    tok = slice((2 * pair + t) * P, (2 * pair + t + 1) * P)
                    for k in range(C):
                        op = mm3(dst[:, t, :], xT_s[0][:, k, tok], xT_s[1][:, k, tok],
                                 wqkv_s[0][:, k, D:3 * D], wqkv_s[1][:, k, D:3 * D], k == 0, k == C - 1)
                op.then_inc(S["a_kv"], 1)

            def a_km(b):
                pe.wait_ge(S["a_k_lo"], at(b, 2, 2))
                pe.wait_ge(S["a_v_lo"], at(b, 2, 2))
                for c in range(C):
                    ch = slice(c * P, (c + 1) * P)
                    for t in range(T):
                        for part in range(2):
                            pe.matmul(Y[:, c, P:P + 2], k_s[part][:, t, ch], ones_r[:], start=(t == 0 and part == 0),
                                      stop=(t == T - 1 and part == 1), skip_group_check=True)
                    for t in range(T):
                        op = mm3(Y[:, c, 0:P], v_s[0][:, t, ch], v_s[1][:, t, ch], k_s[0][:, t, ch], k_s[1][:, t, ch],
                                 False, t == T - 1)
                op.then_inc(S["a_km"], 1)

            def a_kvw(b, prev):
                pe.wait_ge(S["a_km_lo"], at(b, 1, 1))
                if prev:
                    pe.wait_ge(S["b3_xT_lo"], at(b - 1, 1, 0))
                for c in range(C):
                    op = mm3(X[:, c, 0:D], km_s[0][:, c, :], km_s[1][:, c, :], wout_s[0][:, c, :], wout_s[1][:, c, :],
                             True, True)
                op.then_inc(S["a_kvw"], 1)
                pe.wait_ge(S["a_q_lo"], at(b, 1, 1))
                for c in range(C):
                    op = mm3(Y[:, c, :], km_s[0][:, C + c, :], km_s[1][:, C + c, :], qT_s[0][:, c, :], qT_s[1][:, c, :],
                             True, True)
                op.then_inc(S["a_den"], 1)

            def a_out(b):
                pe.wait_ge(S["a_kvw_lo"], at(b, 1, 1))
                pe.wait_ge(S["a_qz_lo"], at(b, 1, 1))
                for pair in range(2):
                    pe.matmul(X[:, pair, :], ones_b[:], bout_rows[:].rearrange("p h n -> p (h n)"),
                              start=True, stop=False, skip_group_check=True)
                    for t in (2 * pair, 2 * pair + 1):
                        for c in range(C):
                            tok = slice(t * P, (t + 1) * P)
                            op = mm3(X[:, pair, (t % 2) * D:(t % 2 + 1) * D], xT_s[0][:, c, tok], xT_s[1][:, c, tok],
                                     kvw_s[0][:, c, :], kvw_s[1][:, c, :], False, c == C - 1)
                op.then_inc(S["a_out"], 1)

            def a1_turn(b):
                pe.wait_ge(S["a1_xn"], at(b, 1, 1))
                turn(X, xn_a, S["a1_xnT"])

            def f_router(r, xs):
                if r is not 0:
                    pe.wait_ge(S["f_y"], at(r, 1, 0))
                for t in range(T):
                    for c in range(C):
                        op = mm3(O[:, 0, t * E:(t + 1) * E], xs[0][:, c, t * P:(t + 1) * P], xs[1][:, c, t * P:(t + 1) * P],
                                 wr_s[0][:, c, :], wr_s[1][:, c, :], t == 0 and c == 0, c == C - 1)
                op.then_inc(S["f_router"], 1)

            def f_h(r, f, xs):
                if not (r is 0 and f < 2):
                    pe.wait_ge(S["f_gelu"], at(r, NF, f - 1))
                ch = slice(f * P, (f + 1) * P)
                for k in range(C):
                    op = mm3(H[f % 2][:], w1_s[0][:, k, ch], w1_s[1][:, k, ch], xs[0][:, k, :], xs[1][:, k, :],
                             k == 0, k == C - 1)
                op.then_inc(S["f_h"], 1)

            def f_o(r, f):
                pe.wait_ge(S["f_h_lo"], at(r, NF, f + 1))
                if f == 0:
                    pe.wait_ge(S["f_top"], at(r, 1, 1))
                    for pair in range(2):
                        pe.matmul(O[:, pair, :], ones_b[:], b2_rows[:].rearrange("p h n -> p (h n)"),
                                  start=True, stop=False, skip_group_check=True)
                h_hi, h_lo = h_s[f % HR]
                for t in range(T):
                    tok = slice(t * P, (t + 1) * P)
                    op = mm3(O[:, t // 2, (t % 2) * D:(t % 2 + 1) * D], h_hi[:, tok], h_lo[:, tok],
                             w2_s[0][:, f, :], w2_s[1][:, f, :], False, f == NF - 1)
                op.then_inc(S["f_o"], 1)

            def b_turn(b):
                pe.wait_ge(S["b_xn"], at(b, 1, 1))
                turn(Y, xn_b, S["b_xnT"])

            def b_kqv(b, t):
                dst = (Y, X)[t % 2]
                if t == 0:
                    pe.wait_ge(S["b_xT_hi"], at(b, 1, 1))
                    pe.wait_ge(S["b_xT_lo"], at(b, 1, 1))
                elif t == 1:
                    if not (b is NB - 1):
                        pe.wait_ge(S["a1_xT_lo"], at(b, 1, 2))
                    else:
                        pe.wait_ge(S["b3_xT_lo"], at(b, 1, 0))
                else:
                    pe.wait_ge(S["b_kqv_n"], at(b, T, t - 1))
                tok = slice(t * P, (t + 1) * P)
                for bank, col, width in ((0, 0, 2 * D), (1, 2 * D, D)):
                    cols = slice(col, col + width)
                    pe.matmul(dst[:, bank, 0:width], ones_b[:], bkqv_rows[:, cols], start=True, stop=False,
                              skip_group_check=True)
                    for k in range(C):
                        op = mm3(dst[:, bank, 0:width], xT_s[0][:, k, tok], xT_s[1][:, k, tok],
                                 wkqv_s[0][:, k, cols], wkqv_s[1][:, k, cols], False, k == C - 1)
                op.then_inc(S["b_kqv"], 1)

            def b_kq_turn(b, which):
                dst, done = ((Y, S["b_kT"]), (X, S["b_qT"]))[which]
                pe.wait_ge(S["b_kqv_n"], at(b, T, T))
                turn(dst, kq_n[:, :, which * D:(which + 1) * D], done)

            def b_scores(b, pair):
                dst = (Y, X)[pair]
                if pair == 0:
                    pe.wait_ge(S["b_kT_lo"], at(b, 1, 1))
                    pe.wait_ge(S["b_qT_lo"], at(b, 1, 1))
                for t in range(2):
                    tok = slice((2 * pair + t) * P, (2 * pair + t + 1) * P)
                    for c in range(C):
                        op = mm3(dst[:, t, :], kqT_s[0][:, c, tok], kqT_s[1][:, c, tok],
                                 kqT_s[0][:, C + c, :], kqT_s[1][:, C + c, :], c == 0, c == C - 1)
                op.then_inc(S["b_sc"], 1)

            def b_prob_turn(b, pair):
                dst = (Y, X)[pair]
                pe.wait_ge(S["b_prob"], at(b, T, T))
                for j in range(2):
                    keys = slice((2 * pair + j) * P, (2 * pair + j + 1) * P)
                    for t in range(T):
                        op = pe.transpose(dst[:, j, t * P:(t + 1) * P], kq_n[:, t, keys], ident[:])
                op.then_inc(S["b_pT"], 1)

            def b_out(b):
                pe.wait_ge(S["b_pT_lo"], at(b, 2, 2))
                pe.wait_ge(S["b_v_lo"], at(b, 1, 1))
                for t in range(T):
                    tok = slice(t * P, (t + 1) * P)
                    for j in range(T):
                        op = mm3(Y[:, t // 2, (t % 2) * D:(t % 2 + 1) * D], kqT_s[0][:, j, tok], kqT_s[1][:, j, tok],
                                 v_s[0][:, j, :], v_s[1][:, j, :], t % 2 == 0 and j == 0, j == T - 1)
                op.then_inc(S["b_out"], 1)

            def b3_turn(b):
                pe.wait_ge(S["b3_xn"], at(b, 1, 1))
                turn(X, xn_b, S["b3_xnT"])

            def phase_1(i, has_a, has_prev, r):
                f_h(r, 0, x1T_s)
                f_router(r, x1T_s)
                f_h(r, 1, x1T_s)
                if has_prev:
                    b_out(i - 1)
                if has_a:
                    a_turn(i + 1, has_prev)
                f_h(r, 2, x1T_s)
                f_o(r, 0)
                if has_a:
                    a_q(i + 1, has_prev)
                    a_kv(i + 1, 0)
                    a_kv(i + 1, 1)
                f_h(r, 3, x1T_s)
                f_o(r, 1)
                if has_prev:
                    if has_a:
                        pe.wait_ge(S["a_v_lo"], at(i + 1, 2, 1))
                    b3_turn(i - 1)
                f_h(r, 4, x1T_s)
                f_o(r, 2)
                if has_a:
                    a_km(i + 1)
                f_h(r, 5, x1T_s)
                f_o(r, 3)
                if has_a:
                    a_kvw(i + 1, has_prev)
                f_h(r, 6, x1T_s)
                f_o(r, 4)
                f_h(r, 7, x1T_s)
                f_o(r, 5)
                f_o(r, 6)
                f_o(r, 7)

            def phase_2(i, has_a, has_prev, r):
                if has_prev:
                    pe.wait_ge(S["b3_xT_lo"], at(i, 1, 0))
                    f_h(r, 0, x3T_s)
                    f_router(r, x3T_s)
                    f_h(r, 1, x3T_s)
                if has_a:
                    a_out(i + 1)
                if has_prev:
                    f_h(r, 2, x3T_s)
                    f_o(r, 0)
                b_turn(i)
                if has_prev:
                    f_h(r, 3, x3T_s)
                    f_o(r, 1)
                if has_a:
                    a1_turn(i + 1)
                b_kqv(i, 0)
                b_kqv(i, 1)
                if has_prev:
                    f_h(r, 4, x3T_s)
                    f_o(r, 2)
                b_kqv(i, 2)
                b_kqv(i, 3)
                if has_prev:
                    f_h(r, 5, x3T_s)
                    f_o(r, 3)
                b_kq_turn(i, 0)
                b_kq_turn(i, 1)
                if has_prev:
                    f_h(r, 6, x3T_s)
                    f_o(r, 4)
                b_scores(i, 0)
                b_scores(i, 1)
                if has_prev:
                    f_h(r, 7, x3T_s)
                    f_o(r, 5)
                    f_o(r, 6)
                b_prob_turn(i, 0)
                b_prob_turn(i, 1)
                if has_prev:
                    f_o(r, 7)

            pe.wait_ge(S["pool_const"], 8)
            a_turn(0, False)
            pe.wait_ge(S["w_lo"], NWT)
            pe.wait_ge(S["bias_rows"], 15 * 16)
            a_q(0, False)
            a_kv(0, 0)
            a_kv(0, 1)
            a_km(0)
            a_kvw(0, False)
            a_out(0)
            a1_turn(0)
            pe.wait_ge(S["a1_xT_lo"], 1)
            phase_1(0, True, False, 0)
            phase_2(0, True, False, 0)
            with pe.Fori(1, NB - 1) as loop_i:
                i, run = turns(pe, loop_i)
                phase_1(i, True, True, run)
                phase_2(i, True, True, run + 1)
            phase_1(NB - 1, False, True, 2 * NB - 3)
            phase_2(NB - 1, False, True, 2 * NB - 2)
            b_out(NB - 1)
            b3_turn(NB - 1)
            pe.wait_ge(S["b3_xT_lo"], NB)
            r = 2 * NB - 1
            f_h(r, 0, x3T_s)
            f_router(r, x3T_s)
            f_h(r, 1, x3T_s)
            for f in range(NF):
                if f + 2 < NF:
                    f_h(r, f + 2, x3T_s)
                f_o(r, f)

        @block.scalar
        def _(act):
            def take_hi(dst, src, ready, value, done):
                act.wait_ge(ready, value)
                act.activation(dst, src, ACT.Copy).then_inc(done, 1)

            def elu_parts(exp_dst, relu_dst, src, exp_done, relu_done):
                act.activation(exp_dst, src, ACT.Exp).then_inc(exp_done, 1)
                act.activation(relu_dst, src, ACT.Relu).then_inc(relu_done, 1)

            def a_q(b):
                act.wait_ge(S["a_q"], at(b, 1, 1))
                elu_parts(tmp[:], q_f[:], Y[:], S["a_q_exp"], S["a_q_relu"])

            def a_kv(b, pair):
                src = (X, Y)[pair]
                act.wait_ge(S["a_kv"], at(b, 2, pair + 1))
                if pair == 0:
                    act.wait_ge(S["a_q_f"], at(b, 1, 1))
                half = tmp[:, pair, :].rearrange("p (t d) -> p t d", t=2)
                tiles = slice(2 * pair, 2 * pair + 2)
                elu_parts(half, k_f[:, tiles, :], src[:, :, 0:D], S["a_kv_exp"], S["a_kv_relu"])
                act.activation(v_s[0][:, tiles, :], src[:, :, D:2 * D], ACT.Copy).then_inc(S["a_v_hi"], 1)

            def a_kvw(b):
                take_hi(kvw_s[0][:], X[:, :, 0:D], S["a_kvw"], at(b, 1, 1), S["a_kvw_hi"])
                act.wait_ge(S["a_den"], at(b, 1, 1))
                act.activation(tmp[:], Y[:], ACT.Identity, bias=z_eps[:, 0:1]).then_inc(S["a_den_eps"], 1)

            def f_gelu(r, f):
                act.wait_ge(S["f_h"], at(r, NF, f + 1))
                if not (r is 0 and f < 2):
                    act.wait_ge(S["f_h_lo"], at(r, NF, f - 1))
                act.activation(h_f[f % 2][:], H[f % 2][:], ACT.Gelu_apprx_tanh, bias=b1_sb[:, f:f + 1]) \
                    .then_inc(S["f_gelu"], 1)

            def f_exp(r):
                act.wait_ge(S["f_shift"], at(r, 1, 1))
                act.activation(top_p[:], top_p[:], ACT.Exp).then_inc(S["f_exp"], 1)

            def b_kq_gain(b, which):
                src, dst = ((Y, tmp), (X, q_f))[which]
                act.wait_ge(S[("b_kT", "b_qT")[which]], at(b, 1, 1))
                for c in range(C):
                    g = 2 * C * which + c
                    act.activation(dst[:, c, :], src[:, c, :], ACT.Identity, bias=kq_gain_sb[:, g + C:g + C + 1],
                                   scale=kq_gain_sb[:, g:g + 1]).then_inc(S[("b_kT_f", "b_qT_f")[which]], 1)

            def b_exp(b, t):
                src = (Y, X)[t // 2]
                act.wait_ge(S["b_max"], at(b, 2, t // 2 + 1))
                act.activation(kq_n[:, t, :], src[:, t % 2, :], ACT.Exp, bias=row_negmax[:, t:t + 1],
                               accum_out=row_sum[:, t:t + 1]).then_inc(S["b_prob"], 1)

            def phase_1(i, has_a, has_prev, r):
                f_gelu(r, 0)
                f_gelu(r, 1)
                if has_a:
                    take_hi(xT_s[0][:], X[:], S["a_xnT"], at(i + 1, 1, 1), S["a_xT_hi"])
                f_gelu(r, 2)
                if has_a:
                    a_q(i + 1)
                    a_kv(i + 1, 0)
                    a_kv(i + 1, 1)
                f_exp(r)
                f_gelu(r, 3)
                if has_prev:
                    take_hi(x3T_s[0][:], X[:], S["b3_xnT"], at(i, 1, 0), S["b3_xT_hi"])
                f_gelu(r, 4)
                f_gelu(r, 5)
                if has_a:
                    a_kvw(i + 1)
                f_gelu(r, 6)
                f_gelu(r, 7)

            def phase_2(i, has_a, has_prev, r):
                if has_prev:
                    f_gelu(r, 0)
                    f_gelu(r, 1)
                    f_gelu(r, 2)
                take_hi(xT_s[0][:], Y[:], S["b_xnT"], at(i, 1, 1), S["b_xT_hi"])
                if has_prev:
                    f_gelu(r, 3)
                if has_a:
                    take_hi(x1T_s[0][:], X[:], S["a1_xnT"], at(i, 1, 2), S["a1_xT_hi"])
                if has_prev:
                    f_gelu(r, 4)
                    f_gelu(r, 5)
                b_kq_gain(i, 0)
                b_kq_gain(i, 1)
                if has_prev:
                    f_gelu(r, 6)
                for t in range(T):
                    b_exp(i, t)
                if has_prev:
                    f_exp(r)
                    f_gelu(r, 7)
                for pair in range(2):
                    take_hi(kqT_s[0][:, 2 * pair:2 * pair + 2, :], (Y, X)[pair][:], S["b_pT"], at(i, 2, pair + 1),
                            S["b_pT_hi"])

            act.wait_ge(S["small_in"], 3 * 16)
            act.wait_ge(S["pool_const"], 8)
            take_hi(xT_s[0][:], X[:], S["a_xnT"], 1, S["a_xT_hi"])
            for n, (src, dst, view) in enumerate(places):
                act.wait_ge(S["w_in"], 16 * NWT)
                act.activation(dst[0][:], view, ACT.Copy).then_inc(S["w_hi"], 1)
            a_q(0)
            a_kv(0, 0)
            a_kv(0, 1)
            a_kvw(0)
            take_hi(x1T_s[0][:], X[:], S["a1_xnT"], 1, S["a1_xT_hi"])
            phase_1(0, True, False, 0)
            phase_2(0, True, False, 0)
            with act.Fori(1, NB - 1) as loop_i:
                i, run = turns(act, loop_i)
                phase_1(i, True, True, run)
                phase_2(i, True, True, run + 1)
            phase_1(NB - 1, False, True, 2 * NB - 3)
            phase_2(NB - 1, False, True, 2 * NB - 2)
            take_hi(x3T_s[0][:], X[:], S["b3_xnT"], NB, S["b3_xT_hi"])
            f_gelu(2 * NB - 1, 0)
            f_exp(2 * NB - 1)
            for f in range(1, NF):
                f_gelu(2 * NB - 1, f)

        @block.vector
        def _(dve):

            dve_places = iter(range(SPARE))

            def carry():
                n = next(dve_places)
                dve.memset(spare_dve[:, n:n + 1], 0.0)

            def take_lo(dst, src, hi, ready, value, done):
                dve.wait_ge(ready, value)
                dve.tensor_tensor(dst, src, hi.bitcast(F32), ALU.subtract).then_inc(done, 1)

            def norm(b, pre, src, dst, st, mv, rs):
                for t in range(T):
                    op = dve.bn_stats(st[:, t, :], src[:, t, :])
                op.then_inc(S[f"{pre}_stats"], 1)
                dve.wait_ge(S[f"{pre}_stats"], at(b, 1, 1))
                carry()
                for t in range(T):
                    op = dve.bn_aggr(mv[:, t, :], st[:, t, :])
                op.then_inc(S[f"{pre}_mv"], 1)
                dve.wait_ge(S[f"{pre}_rstd"], at(b, 1, 1))
                for t in range(T):
                    op = dve.tensor_scalar(dst[:, t, :], src[:, t, :], mv[:, t, 0:1], rs[:, t:t + 1],
                                           ALU.subtract, ALU.mult)
                op.then_inc(S[f"{pre}_xn"], 1)

            def a_norm(b):
                dve.wait_ge(S["x_in"], at(b, 16, 16))
                if b is not 0:
                    dve.wait_ge(S["a1_xnT"], at(b, 1, 0))
                norm(b, "a", x_in, xn_a, stA, mvA, rsA)

            def elu(dst, exp, exp_done, relu_done, value, done):
                dve.wait_ge(relu_done, value)
                dve.wait_ge(exp_done, value)
                dve.scalar_tensor_tensor(dst, exp, 1.0, dst, ALU.min, ALU.add).then_inc(done, 1)

            def a_q(b):
                elu(q_f[:], tmp[:], S["a_q_exp"], S["a_q_relu"], at(b, 1, 1), S["a_q_f"])

            def a_q_lo(b):
                take_lo(qT_s[1][:], q_f[:], qT_s[0][:], S["a_q_hi"], at(b, 1, 1), S["a_q_lo"])

            def a_k(b, pair):
                tiles = slice(2 * pair, 2 * pair + 2)
                half = tmp[:, pair, :].rearrange("p (t d) -> p t d", t=2)
                elu(k_f[:, tiles, :], half, S["a_kv_exp"], S["a_kv_relu"], at(b, 2, pair + 1), S["a_k_f"])
                take_lo(v_s[1][:, tiles, :], (X, Y)[pair][:, :, D:2 * D], v_s[0][:, tiles, :],
                        S["a_v_hi"], at(b, 2, pair + 1), S["a_v_lo"])

            def a_k_lo(b, pair):
                tiles = slice(2 * pair, 2 * pair + 2)
                take_lo(k_s[1][:, tiles, :], k_f[:, tiles, :], k_s[0][:, tiles, :],
                        S["a_k_hi"], at(b, 2, pair + 1), S["a_k_lo"])

            def a_km(b):
                dve.wait_ge(S["a_km"], at(b, 1, 1))
                for c in range(C):
                    dve.tensor_tensor(km_f[:, c, :], Y[:, c, 0:P], head_mask[:], ALU.mult)
                for c in range(C):
                    op = dve.tensor_scalar(km_f[:, C + c, :], head_mask[:], Y[:, c, P:P + 1], None, ALU.mult)
                op.then_inc(S["a_km_f"], 1)
                dve.wait_ge(S["a_km_f"], at(b, 1, 1))
                dve.tensor_copy(km_s[0][:], km_f[:]).then_inc(S["a_km_hi"], 1)
                take_lo(km_s[1][:], km_f[:], km_s[0][:], S["a_km_hi"], at(b, 1, 1), S["a_km_lo"])

            def a_kvw(b):
                take_lo(kvw_s[1][:], X[:, :, 0:D], kvw_s[0][:], S["a_kvw_hi"], at(b, 1, 1), S["a_kvw_lo"])

            def a_z(b, c):
                if c == 0:
                    dve.wait_ge(S["a_den_eps"], at(b, 1, 1))
                dve.reciprocal(tmp[:, c, :], tmp[:, c, :]).then_inc(S["a_z"], 1)

            def a_qz(b):
                dve.wait_ge(S["a_z"], at(b, C, C))
                dve.tensor_tensor(q_f[:], q_f[:], tmp[:], ALU.mult).then_inc(S["a_qz"], 1)

            def a_qz_lo(b):
                take_lo(xT_s[1][:], q_f[:], xT_s[0][:], S["a_qz_hi"], at(b, 1, 1), S["a_qz_lo"])

            def a_x1(b):
                dve.wait_ge(S["a_out"], at(b, 1, 1))
                if b is not 0:
                    dve.wait_ge(S["f_y"], at(b, 2, -2) if b is not 1 else 1)
                dve.tensor_tensor(x1[:].rearrange("p (a t) d -> p a (t d)", a=2), X[:],
                                  x_in[:].rearrange("p (a t) d -> p a (t d)", a=2), ALU.add).then_inc(S["a_x1"], 1)
                dve.wait_ge(S["a_x1"], at(b, 1, 1))
                norm(b, "a1", x1, xn_a, stA, mvA, rsA)

            def f_top(r):
                dve.wait_ge(S["f_router"], at(r, 1, 1))
                carry()
                for t in range(T):
                    op = dve.max(top[:, t, :], O[:, 0, t * E:(t + 1) * E])
                op.then_inc(S["f_top"], 1)
                dve.wait_ge(S["f_top"], at(r, 1, 1))
                dve.tensor_tensor(top_p[:], top[:], top[:, :, 0:1].to_broadcast([P, T, E]), ALU.subtract) \
                    .then_inc(S["f_shift"], 1)

            def f_comb(r):
                dve.wait_ge(S["f_exp"], at(r, 1, 1))
                dve.tensor_reduce(p_sum[:], top_p[:], X_AXIS, ALU.add).then_inc(S["f_psum"], 1)
                dve.wait_ge(S["f_psum"], at(r, 1, 1))
                dve.reciprocal(p_rec[:], p_sum[:]).then_inc(S["f_prec"], 1)
                dve.wait_ge(S["f_prec"], at(r, 1, 1))
                dve.tensor_tensor(p2[:], top_p[:, :, 0:2], p_rec[:].unsqueeze(2).to_broadcast([P, T, 2]), ALU.mult) \
                    .then_inc(S["f_p2"], 1)
                dve.wait_ge(S["f_p2"], at(r, 1, 1))
                dve.tensor_tensor(t_sum[:], p2[:, :, 0], p2[:, :, 1], ALU.add).then_inc(S["f_tsum"], 1)
                dve.wait_ge(S["f_tsum"], at(r, 1, 1))
                dve.reciprocal(t_rec[:], t_sum[:]).then_inc(S["f_trec"], 1)
                dve.wait_ge(S["f_trec"], at(r, 1, 1))
                dve.tensor_tensor(p2[:], p2[:], t_rec[:].unsqueeze(2).to_broadcast([P, T, 2]), ALU.mult) \
                    .then_inc(S["f_comb_p"], 1)
                dve.wait_ge(S["f_comb_p"], at(r, 1, 1))
                dve.tensor_tensor(comb[:], p2[:, :, 0], p2[:, :, 1], ALU.add).then_inc(S["f_comb"], 1)

            def f_lo(r, f):
                if not (r is 0 and f < HR):
                    dve.wait_ge(S["f_o"], at(r, NF, f + 1 - HR))
                take_lo(h_s[f % HR][1][:], h_f[f % 2][:], h_s[f % HR][0][:], S["f_h_hi"], at(r, NF, f + 1), S["f_h_lo"])

            def f_y(r, res, dst):
                dve.wait_ge(S["f_comb"], at(r, 1, 1))
                dve.wait_ge(S["f_o"], at(r, NF, NF))
                for t in range(T):
                    op = dve.scalar_tensor_tensor(dst[:, t, :], O[:, t // 2, (t % 2) * D:(t % 2 + 1) * D],
                                                  comb[:, t:t + 1], res[:, t, :], ALU.mult, ALU.add)
                op.then_inc(S["f_y"], 1)

            def b_norm(b, has_prev):
                dve.wait_ge(S["f_y"], at(b, 2, 0) if has_prev else 1)
                if has_prev:
                    dve.wait_ge(S["b3_xnT"], at(b, 1, 0))
                norm(b, "b", x2, xn_b, stF, mvF, rsF)

            def b_kqv(b, t):
                src = (Y, X)[t % 2]
                parts = (src[:, 0, 0:D], src[:, 0, D:2 * D], src[:, 1, 0:D])
                dve.wait_ge(S["b_kqv"], at(b, T, t + 1))
                for n in range(3):
                    op = dve.bn_stats(stK[:, t, n, :], parts[n])
                op.then_inc(S["b_kqv_stats"], 1)
                dve.wait_ge(S["b_kqv_stats"], at(b, T, t + 1))
                carry()
                for n in range(3):
                    op = dve.bn_aggr(mvK[:, t, n, :], stK[:, t, n, :])
                op.then_inc(S["b_kqv_mv"], 1)

            def b_kqv_n(b, t):
                src = (Y, X)[t % 2]
                dsts = (kq_n[:, t, 0:D], kq_n[:, t, D:2 * D], v_f[:, t, :])
                parts = (src[:, 0, 0:D], src[:, 0, D:2 * D], src[:, 1, 0:D])
                dve.wait_ge(S["b_kqv_rstd"], at(b, T, t + 1))
                if t == 0:
                    pass
                for n in range(3):
                    op = dve.tensor_scalar(dsts[n], parts[n], mvK[:, t, n, 0:1], rsK[:, t, n:n + 1],
                                           ALU.subtract, ALU.mult)
                op.then_inc(S["b_kqv_n"], 1)

            def b_kq_lo(b, which):
                src = (tmp, q_f)[which]
                n = ("k", "q")[which]
                take_lo(kqT_s[1][:, C * which:C * which + C, :], src[:], kqT_s[0][:, C * which:C * which + C, :],
                        S[f"b_{n}T_hi"], at(b, 1, 1), S[f"b_{n}T_lo"])

            def b_v_lo(b):
                take_lo(v_s[1][:], v_f[:], v_s[0][:], S["b_v_hi"], at(b, 1, 1), S["b_v_lo"])

            def b_max(b, pair):
                dve.wait_ge(S["b_sc"], at(b, 2, pair + 1))
                dve.tensor_reduce(row_negmax[:, 2 * pair:2 * pair + 2], (Y, X)[pair][:], X_AXIS, ALU.max,
                                  negate=True).then_inc(S["b_max"], 1)

            def b_pT_lo(b, pair):
                js = slice(2 * pair, 2 * pair + 2)
                take_lo(kqT_s[1][:, js, :], (Y, X)[pair][:], kqT_s[0][:, js, :], S["b_pT_hi"], at(b, 2, pair + 1),
                        S["b_pT_lo"])

            def b_x3(b):
                dve.wait_ge(S["b_prob"], at(b, T, T))
                dve.reciprocal(row_rec[:], row_sum[:]).then_inc(S["b_rec"], 1)
                dve.wait_ge(S["b_rec"], at(b, 1, 1))
                dve.wait_ge(S["b_res"], at(b, 1, 1))
                if not (b is 0):
                    dve.wait_ge(S["x_out"], at(b, 16, 16))
                dve.wait_ge(S["b_out"], at(b, 1, 1))
                for t in range(T):
                    op = dve.scalar_tensor_tensor(x3[:, t, :], Y[:, t // 2, (t % 2) * D:(t % 2 + 1) * D],
                                                  row_rec[:, t:t + 1], x2[:, t, :], ALU.mult, ALU.add)
                op.then_inc(S["b_x3"], 1)
                dve.wait_ge(S["b_x3"], at(b, 1, 1))
                norm(b, "b3", x3, xn_b, stF, mvF, rsF)

            def xT_lo(dst, src, hi, pre, b):
                take_lo(dst[:], src[:], hi[:], S[f"{pre}_xT_hi"], at(b, 1, 1), S[f"{pre}_xT_lo"])

            def phase_1(i, has_a, has_prev, r):
                if has_a:
                    a_norm(i + 1)
                f_lo(r, 0)
                f_top(r)
                f_lo(r, 1)
                if has_a:
                    xT_lo(xT_s[1], X, xT_s[0], "a", i + 1)
                if has_prev:
                    b_x3(i - 1)
                f_lo(r, 2)
                if has_a:
                    a_q(i + 1)
                    a_q_lo(i + 1)
                    a_k(i + 1, 0)
                    a_k_lo(i + 1, 0)
                    a_k(i + 1, 1)
                    a_k_lo(i + 1, 1)
                f_lo(r, 3)
                f_comb(r)
                if has_prev:
                    xT_lo(x3T_s[1], X, x3T_s[0], "b3", i - 1)
                f_lo(r, 4)
                if has_a:
                    a_km(i + 1)
                f_lo(r, 5)
                if has_a:
                    a_kvw(i + 1)
                    a_z(i + 1, 0)
                f_lo(r, 6)
                if has_a:
                    a_z(i + 1, 1)
                f_lo(r, 7)
                if has_a:
                    a_qz(i + 1)
                f_y(r, x1, x2)
                if has_a:
                    a_qz_lo(i + 1)
                b_norm(i, has_prev)

            def phase_2(i, has_a, has_prev, r):
                if has_prev:
                    f_lo(r, 0)
                    f_top(r)
                    f_lo(r, 1)
                if has_a:
                    a_x1(i + 1)
                if has_prev:
                    f_lo(r, 2)
                xT_lo(xT_s[1], Y, xT_s[0], "b", i)
                if has_prev:
                    f_lo(r, 3)
                if has_a:
                    xT_lo(x1T_s[1], X, x1T_s[0], "a1", i + 1)
                b_kqv(i, 0)
                b_kqv(i, 1)
                b_kqv_n(i, 0)
                b_kqv_n(i, 1)
                if has_prev:
                    f_lo(r, 4)
                b_kqv(i, 2)
                b_kqv(i, 3)
                b_kqv_n(i, 2)
                b_kqv_n(i, 3)
                if has_prev:
                    f_lo(r, 5)
                b_kq_lo(i, 0)
                b_kq_lo(i, 1)
                if has_prev:
                    f_lo(r, 6)
                b_max(i, 0)
                b_max(i, 1)
                if has_prev:
                    f_lo(r, 7)
                    f_comb(r)
                b_v_lo(i)
                b_pT_lo(i, 0)
                b_pT_lo(i, 1)
                if has_prev:
                    f_y(r, x3, x3)

            dve.wait_ge(S["bias_in"], 3 * 16)
            dve.tensor_copy(bias_b[0:1, 0, :], bias_f[:]).then_inc(S["bias_part"], 1)
            for n in range(1, 3):
                dve.wait_ge(S["bias_part"], 2 * n - 1)
                dve.tensor_tensor(bias_f[:], bias_f[:], bias_b[0:1, n - 1, :], ALU.subtract) \
                    .then_inc(S["bias_part"], 1)
                dve.wait_ge(S["bias_part"], 2 * n)
                dve.tensor_copy(bias_b[0:1, n, :], bias_f[:]).then_inc(S["bias_part"], 1)
            dve.memset(z_eps[:], 1e-6).then_inc(S["bias_part"], 1)
            a_norm(0)
            xT_lo(xT_s[1], X, xT_s[0], "a", 0)
            for n, (src, dst, view) in enumerate(places):
                take_lo(dst[1][:], view, dst[0][:], S["w_hi"], n + 1, S["w_lo"])
            a_q(0)
            a_q_lo(0)
            for pair in range(2):
                a_k(0, pair)
                a_k_lo(0, pair)
            a_km(0)
            a_kvw(0)
            a_z(0, 0)
            a_z(0, 1)
            a_qz(0)
            a_qz_lo(0)
            a_x1(0)
            xT_lo(x1T_s[1], X, x1T_s[0], "a1", 0)
            phase_1(0, True, False, 0)
            phase_2(0, True, False, 0)
            with dve.Fori(1, NB - 1) as loop_i:
                i, run = turns(dve, loop_i)
                phase_1(i, True, True, run)
                phase_2(i, True, True, run + 1)
            phase_1(NB - 1, False, True, 2 * NB - 3)
            phase_2(NB - 1, False, True, 2 * NB - 2)
            b_x3(NB - 1)
            xT_lo(x3T_s[1], X, x3T_s[0], "b3", NB - 1)
            r = 2 * NB - 1
            f_lo(r, 0)
            f_top(r)
            f_lo(r, 1)
            f_comb(r)
            for f in range(2, NF):
                f_lo(r, f)
            f_y(r, x3, x3)

        @block.gpsimd
        def _(pool):

            pool_places = iter(range(SPARE))

            def carry():
                n = next(pool_places)
                pool.tensor_tensor(spare_pool[:, n:n + 1], neg_half[:, 0:1], neg_half[:, 0:1], ALU.mult)

            def rstd(dst, ve, mv, pre, count, width):
                pool.wait_ge(S[f"{pre}_mv"], count)
                carry()
                pool.tensor_scalar(ve, mv, EPS, None, ALU.add).then_inc(S[f"{pre}_ve"], 1)
                pool.wait_ge(S[f"{pre}_ve"], count)
                pool.tensor_tensor(dst, ve, neg_half[:, 0:width], ALU.pow).then_inc(S[f"{pre}_rstd"], 1)

            def norm_rstd(b, pre, ve, mv, rs):
                rstd(rs[:], ve[:], mv[:, :, 1], pre, at(b, 1, 1), T)

            def take_hi(dst, src, ready, value, done):
                pool.wait_ge(ready, value)
                carry()
                pool.tensor_copy(dst, src).then_inc(done, 1)

            def a_q_hi(b):
                take_hi(qT_s[0][:], q_f[:], S["a_q_f"], at(b, 1, 1), S["a_q_hi"])

            def a_k_hi(b, pair):
                tiles = slice(2 * pair, 2 * pair + 2)
                take_hi(k_s[0][:, tiles, :], k_f[:, tiles, :], S["a_k_f"], at(b, 2, pair + 1), S["a_k_hi"])

            def a_qz_hi(b):
                take_hi(xT_s[0][:], q_f[:], S["a_qz"], at(b, 1, 1), S["a_qz_hi"])

            def f_hi(r, f):
                if not (r is 0 and f < HR):
                    pool.wait_ge(S["f_o"], at(r, NF, f + 1 - HR))
                take_hi(h_s[f % HR][0][:], h_f[f % 2][:], S["f_gelu"], at(r, NF, f + 1), S["f_h_hi"])

            def b_res(b):
                pool.wait_ge(S["b_xn"], at(b, 1, 1))
                pool.tensor_tensor(x2[:], x2[:], xn_b[:], ALU.add).then_inc(S["b_res"], 1)

            def b_kqv_rstd(b, t):
                rstd(rsK[:, t, :], veK[:, t, :], mvK[:, t, :, 1], "b_kqv", at(b, T, t + 1), 3)

            def b_kq_hi(b, which):
                n = ("k", "q")[which]
                take_hi(kqT_s[0][:, C * which:C * which + C, :], (tmp, q_f)[which][:], S[f"b_{n}T_f"], at(b, C, C),
                        S[f"b_{n}T_hi"])

            def b_v(b):
                pool.wait_ge(S["b_kqv_n"], at(b, T, T))
                pool.tensor_tensor(v_f[:], v_f[:], v_gain_sb[:].unsqueeze(1).to_broadcast([P, T, D]), ALU.mult) \
                    .then_inc(S["b_v_g"], 1)
                pool.wait_ge(S["b_v_g"], at(b, 1, 1))
                pool.tensor_tensor(v_f[:], v_f[:], v_beta_sb[:].unsqueeze(1).to_broadcast([P, T, D]), ALU.add) \
                    .then_inc(S["b_v_f"], 1)
                take_hi(v_s[0][:], v_f[:], S["b_v_f"], at(b, 1, 1), S["b_v_hi"])

            def phase_1(i, has_a, has_prev, r):
                if has_a:
                    norm_rstd(i + 1, "a", veA, mvA, rsA)
                f_hi(r, 0)
                f_hi(r, 1)
                if has_prev:
                    norm_rstd(i - 1, "b3", veF, mvF, rsF)
                f_hi(r, 2)
                if has_a:
                    a_q_hi(i + 1)
                    a_k_hi(i + 1, 0)
                    a_k_hi(i + 1, 1)
                for f in range(3, NF):
                    f_hi(r, f)
                if has_a:
                    a_qz_hi(i + 1)
                norm_rstd(i, "b", veF, mvF, rsF)

            def phase_2(i, has_a, has_prev, r):
                if has_prev:
                    f_hi(r, 0)
                    f_hi(r, 1)
                if has_a:
                    norm_rstd(i + 1, "a1", veA, mvA, rsA)
                if has_prev:
                    f_hi(r, 2)
                    f_hi(r, 3)
                b_res(i)
                b_kqv_rstd(i, 0)
                b_kqv_rstd(i, 1)
                if has_prev:
                    f_hi(r, 4)
                b_kqv_rstd(i, 2)
                b_kqv_rstd(i, 3)
                if has_prev:
                    f_hi(r, 5)
                b_kq_hi(i, 0)
                b_kq_hi(i, 1)
                if has_prev:
                    f_hi(r, 6)
                    f_hi(r, 7)
                b_v(i)

            done = 0

            def const(op):
                nonlocal done
                op.then_inc(S["pool_const"], 1)
                done += 1
                pool.wait_ge(S["pool_const"], done)

            for rows in (bout_rows, b2_rows, bkqv_rows):
                pool.memset(rows[:], 0.0).then_inc(S["zeroed"], 1)
            const(pool.memset(ident[:], 0.0))
            const(pool.affine_select(out=ident[:], in_=ident[:], compare_op=ALU.not_equal, fill=1.0, base=0,
                                     pattern=[[-1, P]], channel_multiplier=1))
            const(pool.memset(head_mask[:], 1.0))
            by_head = head_mask[:].rearrange("p (h d) -> p h d", d=HD)
            const(pool.affine_select(out=by_head, in_=by_head, compare_op=ALU.is_ge, fill=0.0, base=0,
                                     pattern=[[-HD, P // HD], [0, HD]], channel_multiplier=1))
            const(pool.affine_select(out=by_head, in_=by_head, compare_op=ALU.is_ge, fill=0.0, base=HD - 1,
                                     pattern=[[HD, P // HD], [0, HD]], channel_multiplier=-1))
            const(pool.memset(ones_r[:].bitcast(F32), 1.0))
            const(pool.memset(ones_b[:], 1.0))
            const(pool.memset(neg_half[:], -0.5))

            pool.wait_ge(S["small_in"], 3 * 16)
            pool.wait_ge(S["x_out"], 16)
            norm_rstd(0, "a", veA, mvA, rsA)
            a_q_hi(0)
            a_k_hi(0, 0)
            a_k_hi(0, 1)
            a_qz_hi(0)
            norm_rstd(0, "a1", veA, mvA, rsA)
            phase_1(0, True, False, 0)
            phase_2(0, True, False, 0)
            with pool.Fori(1, NB - 1) as loop_i:
                i, run = turns(pool, loop_i)
                phase_1(i, True, True, run)
                phase_2(i, True, True, run + 1)
            phase_1(NB - 1, False, True, 2 * NB - 3)
            phase_2(NB - 1, False, True, 2 * NB - 2)
            norm_rstd(NB - 1, "b3", veF, mvF, rsF)
            for f in range(NF):
                f_hi(2 * NB - 1, f)


def kernel(**inputs):
    import numpy as np
    import concourse.bacc as bacc
    from concourse.bass_utils import run_bass_kernel_spmd

    g = {name: np.asarray(a) for name, a in inputs.items()}

    def cols(v):
        return v.reshape(-1, P).T

    b = "L0_attn_b_"
    arrays = {
        "x": g["L0_attn_a_x"],
        "w_qkv": g["L0_attn_a_w_qkv"].T,
        "w_out": g["L0_attn_a_w_out"].T,
        "b_out": g["L0_attn_a_b_out"].reshape(1, -1),
        "w_kqv": np.concatenate([g[b + "Wk"], g[b + "Wq"], g[b + "Wv"]], axis=1),
        "b_kqv": np.concatenate([g[b + "bk"], g[b + "bq"], g[b + "bv"]]).reshape(1, -1),
        "kq_gain": np.concatenate([cols(g[b + n]) for n in ("gk", "betak", "gq", "betaq")], axis=1),
        "v_gain": g[b + "gv"],
        "v_beta": g[b + "betav"],
        "router_w": g["L0_ffn_router_w"],
        "w1": g["L0_ffn_w1"],
        "b1": cols(g["L0_ffn_b1"]),
        "w2": g["L0_ffn_w2"],
        "b2": g["L0_ffn_b2"].reshape(1, -1),
    }
    arrays = {name: np.ascontiguousarray(a) for name, a in arrays.items()}
    nc = bacc.Bacc("TRN2", target_bir_lowering=False, num_devices=1)
    args = [nc.dram_tensor(name, a.shape, mybir.dt.from_np(a.dtype), kind="ExternalInput").ap()
            for name, a in arrays.items()]
    out = nc.dram_tensor("out", arrays["x"].shape, F32, kind="ExternalOutput").ap()
    hybrid_block(nc, *args, out)
    r = run_bass_kernel_spmd(nc, [arrays], core_ids=[0])
    return r.results[0]["out"]
```

```python
from contextlib import ExitStack

import concourse.bass as bass
from concourse import mybir

F32 = mybir.dt.float32
F32R = mybir.dt.float32r
BF16 = mybir.dt.bfloat16
ALU = mybir.AluOpType
ACT = mybir.ActivationFunctionType
X_AXIS = mybir.AxisListType.X

P = 128
PARTS = ("hi", "lo")


class Turn:

    def __init__(self, multiples, scale, offset):
        self.multiples, self.scale, self.offset = multiples, scale, offset

    def __add__(self, n):
        return Turn(self.multiples, self.scale, self.offset + n)

    def __sub__(self, n):
        return self + -n

    def times(self, n):
        return Turn(self.multiples, self.scale * n, self.offset * n)


def turns(eng, i):
    multiples = {m: eng.snap(i * m) for m in (1, 2, 4, 8, 16)}
    batch = Turn(multiples, 1, 0)
    return batch, batch.times(2) - 1


def at(turn, per_turn, k):
    if isinstance(turn, Turn):
        count = turn.offset * per_turn + k
        value = turn.multiples[turn.scale * per_turn]
        return value + count if count else value
    return turn * per_turn + k


def hybrid_block(nc, x, w_qkv, w_out, b_out, w_kqv, b_kqv, kq_gain, v_gain, v_beta,
                 router_w, w1, b1, w2, b2, out):
    NB, N, D = x.shape
    T = N // P
    C = D // P
    FF = w1.shape[1]
    NF = FF // P
    E = router_w.shape[1]
    HD = 16
    EPS = 1e-5
    assert (T, C, N, E) == (4, 2, 512, 8) and NF == 8

    with ExitStack() as ctx:
        def sb(name, shape, dt=F32, cx=ctx):
            return cx.enter_context(nc.sbuf_tensor(name, shape, dt))

        def split(name, shape):
            return [sb(f"{name}_{part}", shape, F32R) for part in PARTS]

        def sem(name):
            return ctx.enter_context(nc.semaphore(name))

        wqkv_s = split("wqkv", [P, C, 3 * D])
        wout_s = split("wout", [P, C, D])
        wkqv_s = split("wkqv", [P, C, 3 * D])
        wr_s = sb("wr", [P, C, P], F32R)
        w1_s = split("w1", [P, C, FF])
        w2_s = split("w2", [P, NF, D])
        ident = sb("ident", [P, P])
        head_mask = sb("head_mask", [P, P])
        ones_b = sb("ones_b", [P, P], BF16)
        bout_rows = sb("bout_rows", [P, 2, D], BF16)
        b2_rows = sb("b2_rows", [P, 2, D], BF16)
        bkqv_rows = sb("bkqv_rows", [P, 3 * D], BF16)
        kq_gain_sb = sb("kq_gain_sb", [P, 4 * C])
        b1_sb = sb("b1_sb", [P, NF])
        v_gain_sb = sb("v_gain_sb", [P, D])
        v_beta_sb = sb("v_beta_sb", [P, D])
        neg_half = sb("neg_half", [P, 3 * T])
        z_eps = sb("z_eps", [P, 1])
        SPARE = 256
        spare_dve, spare_pool = sb("spare_dve", [P, SPARE], BF16), sb("spare_pool", [P, SPARE], BF16)
        stA, stF, stK = sb("stA", [P, T, 6]), sb("stF", [P, T, 6]), sb("stK", [P, T, 3, 6])
        mvA, mvF, mvK = sb("mvA", [P, T, 2]), sb("mvF", [P, T, 2]), sb("mvK", [P, T, 3, 2])
        rsA, rsF, rsK = sb("rsA", [P, T]), sb("rsF", [P, T]), sb("rsK", [P, T, 3])
        veA, veF, veK = sb("veA", [P, T]), sb("veF", [P, T]), sb("veK", [P, T, 3])
        logits_T = sb("logits_T", [P, N])
        logit_hi = sb("logit_hi", [P, T, E])
        logits = sb("logits", [P, T, E])
        top = sb("top", [P, T, E])
        top_p = sb("top_p", [P, T, E])
        p_sum, p_rec = sb("p_sum", [P, T]), sb("p_rec", [P, T])
        t_sum, t_rec = sb("t_sum", [P, T]), sb("t_rec", [P, T])
        comb = sb("comb", [P, T])
        p2 = sb("p2", [P, T, 2])
        row_negmax, row_sum, row_rec = sb("row_negmax", [P, T]), sb("row_sum", [P, T]), sb("row_rec", [P, T])
        x_in = sb("x_in", [P, T, D])
        xn_a = sb("xn_a", [P, T, D])
        xn_b = sb("xn_b", [P, T, D])
        xT_s = split("xT", [P, C, N])
        q_f = sb("q_f", [P, C, N])
        tmp = sb("tmp", [P, C, N])
        qT_s = split("qT", [P, C, N])
        k_s = split("k", [P, T, D])
        VW = P + 2
        v_s = split("v", [P, T, C, VW])
        v_f = sb("v_f", [P, T, D])
        km_f = sb("km_f", [P, 2 * C, P])
        km_s = split("km", [P, 2 * C, P])
        stage_cx = ExitStack()
        NW = C * 3 * D * 2 + C * D + C * E + C * FF + NF * D
        stage = sb("stage", [P, NW], F32, stage_cx)
        bias_f = sb("bias_f", [1, 5 * D], F32, stage_cx)
        bias_b = sb("bias_b", [1, 3, 5 * D], BF16, stage_cx)
        stage_cx.close()
        x1 = sb("x1", [P, T, D])
        x1T_s = split("x1T", [P, C, N])
        x2 = sb("x2", [P, T, D])
        kq_n = sb("kq_n", [P, T, 2 * D])
        k_f = kq_n[:, :, 0:D]
        kqT_s = split("kqT", [P, 2 * C, N])
        x3 = sb("x3", [P, T, D])
        x3T_s = split("x3T", [P, C, N])
        HR = 4
        h_f = [sb(f"h_f{n}", [P, N]) for n in range(2)]
        h_s = [split(f"h{n}", [P, N]) for n in range(HR)]

        X = ctx.enter_context(nc.psum_tensor("X", [P, 2, 512], F32))
        Y = ctx.enter_context(nc.psum_tensor("Y", [P, 2, 512], F32))
        O = ctx.enter_context(nc.psum_tensor("O", [P, 2, 512], F32))
        H = [ctx.enter_context(nc.psum_tensor(f"H{n}", [P, 512], F32)) for n in range(2)]

        names = """w_in small_in bias_in bias_rows w_hi w_lo consts pool_const zeroed bias_part
        x_in x_out
        a_stats a_mv a_ve a_rstd a_xn a_xnT a_xT_hi a_xT_lo
        a_q a_q_exp a_q_relu a_q_f a_q_hi a_q_lo
        a_kv a_kv_exp a_kv_relu a_k_f a_k_hi a_k_lo a_v_hi a_v_lo
        a_km a_km_f a_km_hi a_km_lo a_att a_den a_den_eps a_z a_attn a_attn_hi a_attn_lo
        a_out a_x1 a1_stats a1_mv a1_ve a1_rstd a1_xn a1_xnT a1_xT_hi a1_xT_lo
        f_router f_logits_T f_router_turn f_logit_hi f_logits f_top f_shift f_exp f_psum f_prec f_p2 f_tsum f_trec f_comb_p f_comb
        f_h f_h_hi f_gelu f_h_lo f_o f_y
        b_stats b_mv b_ve b_rstd b_xn b_res b_xnT b_xT_hi b_xT_lo
        b_kqv b_kqv_stats b_kqv_mv b_kqv_ve b_kqv_rstd b_kqv_n b_v_g b_v_f b_v_hi b_v_lo
        b_kT b_kT_f b_kT_hi b_kT_lo b_qT b_qT_f b_qT_hi b_qT_lo
        b_sc b_max b_prob b_pT b_pT_hi b_pT_lo b_rec b_out b_x3
        b3_stats b3_mv b3_ve b3_rstd b3_xn b3_xnT b3_xT_hi b3_xT_lo""".split()
        S = {n: sem(n) for n in names}

        places, base = [], 0
        for src, dst in ((w_qkv, wqkv_s), (w_out, wout_s),
                         (router_w, [wr_s[:, :, 0:E], wr_s[:, :, E:2 * E]]), (w1, w1_s), (w2, w2_s), (w_kqv, wkqv_s)):
            chunks, width = src.shape[0] // P, src.shape[1]
            view = stage[:, base:base + chunks * width].rearrange("p (c n) -> p c n", c=chunks)
            places.append((src, dst, view))
            base += chunks * width
        NWT = len(places)
        biases = ((b_out, 0, D), (b2, D, D), (b_kqv, 2 * D, 3 * D))

        NCONST = 10

        block = ctx.enter_context(nc.Block())

        @block.sync
        def _(sp):
            def load_x(b, peeled=False):
                if not (peeled and b == 0):
                    sp.wait_ge(S["a_x1"], at(b, 1, 0))
                sp.dma_start(x_in[:], x[bass.ds(b, 1)].rearrange("o (t p) d -> p (o t) d", p=P)) \
                    .then_inc(S["x_in"], 16)

            def store_out(b):
                sp.wait_ge(S["f_y"], 2 * b + 3)
                sp.dma_start(out[bass.ds(b, 1)].rearrange("o (t p) d -> p (o t) d", p=P), x3[:]) \
                    .then_inc(S["x_out"], 16)

            for src, dst, view in places[:1]:
                sp.dma_start(view, src.rearrange("(c p) n -> p c n", p=P)).then_inc(S["w_in"], 16)
            load_x(0, True)
            for src, at0, width in biases:
                sp.dma_start(bias_f[0:1, at0:at0 + width], src).then_inc(S["bias_in"], 16)
            for src, dst, view in places[1:]:
                sp.dma_start(view, src.rearrange("(c p) n -> p c n", p=P)).then_inc(S["w_in"], 16)
            sp.dma_start(kq_gain_sb[:], kq_gain).then_inc(S["small_in"], 16)
            sp.dma_start(b1_sb[:], b1).then_inc(S["small_in"], 16)
            sp.dma_start(v_gain_sb[:], v_gain.partition_broadcast(P)).then_inc(S["small_in"], 16)
            sp.dma_start(v_beta_sb[:], v_beta.partition_broadcast(P)).then_inc(S["x_out"], 16)
            sp.wait_ge(S["bias_part"], 6)
            sp.wait_ge(S["zeroed"], 3)
            for row in range(3):
                for half in range(2):
                    sp.dma_start(bout_rows[row:row + 1, half, :], bias_b[0:1, row, 0:D]).then_inc(S["bias_rows"], 16)
                    sp.dma_start(b2_rows[row:row + 1, half, :], bias_b[0:1, row, D:2 * D]).then_inc(S["bias_rows"], 16)
                sp.dma_start(bkqv_rows[row:row + 1, :], bias_b[0:1, row, 2 * D:5 * D]).then_inc(S["bias_rows"], 16)
            load_x(1)
            load_x(2)
            with sp.Fori(1, NB - 2) as i:
                load_x(i + 2)
                store_out(i - 1)
            store_out(NB - 3)
            store_out(NB - 2)
            sp.wait_ge(S["f_y"], 2 * NB)
            sp.dma_start(out[NB - 1:NB].rearrange("o (t p) d -> p (o t) d", p=P), x3[:]).then_inc(S["x_out"], 16)
            sp.wait_ge(S["x_out"], 16 * (NB + 1))

        @block.tensor
        def _(pe):
            def mm3(dst, l_hi, l_lo, r_hi, r_lo, start, stop):
                pe.matmul(dst, l_hi, r_hi, start=start, stop=False, skip_group_check=True)
                pe.matmul(dst, l_hi, r_lo, start=False, stop=False, skip_group_check=True)
                return pe.matmul(dst, l_lo, r_hi, start=False, stop=stop, skip_group_check=True)

            def turn(dst, src, done):
                for c in range(C):
                    for t in range(T):
                        op = pe.transpose(dst[:, c, t * P:(t + 1) * P], src[:, t, c * P:(c + 1) * P], ident[:])
                op.then_inc(done, 1)

            def a_turn(b, prev):
                pe.wait_ge(S["a_xn"], at(b, 1, 1))
                if prev:
                    pe.wait_ge(S["b_pT_lo"], at(b - 1, 2, 0))
                elif b != 0:
                    pe.wait_ge(S["a1_xT_lo"], at(b, 1, 0))
                turn(X, xn_a, S["a_xnT"])

            def a_q(b, prev):
                pe.wait_ge(S["a_xT_hi"], at(b, 1, 1))
                pe.wait_ge(S["a_xT_lo"], at(b, 1, 1))
                if prev:
                    pe.wait_ge(S["b_x3"], at(b - 1, 1, 0))
                for m in range(C):
                    for k in range(C):
                        op = mm3(Y[:, m, :], wqkv_s[0][:, k, m * P:(m + 1) * P], wqkv_s[1][:, k, m * P:(m + 1) * P],
                                 xT_s[0][:, k, :], xT_s[1][:, k, :], k == 0, k == C - 1)
                op.then_inc(S["a_q"], 1)

            def a_kv(b, pair):
                dst = (X, Y)[pair]
                if pair:
                    pe.wait_ge(S["a_q_relu"], at(b, 1, 1))
                for t in range(2):
                    tok = slice((2 * pair + t) * P, (2 * pair + t + 1) * P)
                    for k in range(C):
                        op = mm3(dst[:, t, :], xT_s[0][:, k, tok], xT_s[1][:, k, tok],
                                 wqkv_s[0][:, k, D:3 * D], wqkv_s[1][:, k, D:3 * D], k == 0, k == C - 1)
                op.then_inc(S["a_kv"], 1)

            def a_km(b):
                pe.wait_ge(S["a_k_lo"], at(b, 2, 2))
                pe.wait_ge(S["a_v_lo"], at(b, 2, 2))
                for c in range(C):
                    ch = slice(c * P, (c + 1) * P)
                    for t in range(T):
                        op = mm3(Y[:, c, 0:VW], k_s[0][:, t, ch], k_s[1][:, t, ch], v_s[0][:, t, c, :], v_s[1][:, t, c, :],
                                 t == 0, t == T - 1)
                op.then_inc(S["a_km"], 1)

            def a_att(b, prev):
                pe.wait_ge(S["a_km_lo"], at(b, 1, 1))
                pe.wait_ge(S["a_q_lo"], at(b, 1, 1))
                if prev:
                    pe.wait_ge(S["b3_xT_lo"], at(b - 1, 1, 0))
                for dst, first, done in ((Y, C, S["a_den"]), (X, 0, S["a_att"])):
                    for c in range(C):
                        op = mm3(dst[:, c, :], km_s[0][:, first + c, :], km_s[1][:, first + c, :],
                                 qT_s[0][:, c, :], qT_s[1][:, c, :], True, True)
                    op.then_inc(done, 1)

            def a_out(b):
                pe.wait_ge(S["a_attn_lo"], at(b, 1, 1))
                for pair in range(2):
                    pe.matmul(X[:, pair, :], ones_b[:], bout_rows[:].rearrange("p h n -> p (h n)"),
                              start=True, stop=False, skip_group_check=True)
                    for t in (2 * pair, 2 * pair + 1):
                        for c in range(C):
                            tok = slice(t * P, (t + 1) * P)
                            op = mm3(X[:, pair, (t % 2) * D:(t % 2 + 1) * D], xT_s[0][:, c, tok], xT_s[1][:, c, tok],
                                     wout_s[0][:, c, :], wout_s[1][:, c, :], False, c == C - 1)
                op.then_inc(S["a_out"], 1)

            def a1_turn(b):
                pe.wait_ge(S["a1_xn"], at(b, 1, 1))
                turn(X, xn_a, S["a1_xnT"])

            def f_router(r, xs):
                if r is not 0:
                    pe.wait_ge(S["f_y"], at(r, 1, 0))
                for c in range(C):
                    for part in range(2):
                        op = pe.matmul(O[:, 0, :], wr_s[:, c, :], xs[part][:, c, :], start=(c == 0 and part == 0),
                                       stop=(c == C - 1 and part == 1))
                op.then_inc(S["f_router"], 1)

            def f_router_turn(r):
                pe.wait_ge(S["f_logits_T"], at(r, 1, 1))
                for t in range(T):
                    op = pe.transpose(O[:, 1, t * P:(t + 1) * P], logits_T[:, t * P:(t + 1) * P], ident[:])
                op.then_inc(S["f_router_turn"], 1)

            def f_h(r, f, xs):
                if not (r is 0 and f < 2):
                    pe.wait_ge(S["f_gelu"], at(r, NF, f - 1))
                ch = slice(f * P, (f + 1) * P)
                for k in range(C):
                    op = mm3(H[f % 2][:], w1_s[0][:, k, ch], w1_s[1][:, k, ch], xs[0][:, k, :], xs[1][:, k, :],
                             k == 0, k == C - 1)
                op.then_inc(S["f_h"], 1)

            def f_o(r, f):
                pe.wait_ge(S["f_h_lo"], at(r, NF, f + 1))
                if f == 0:
                    pe.wait_ge(S["f_logits"], at(r, 1, 1))
                    for pair in range(2):
                        pe.matmul(O[:, pair, :], ones_b[:], b2_rows[:].rearrange("p h n -> p (h n)"),
                                  start=True, stop=False, skip_group_check=True)
                h_hi, h_lo = h_s[f % HR]
                for t in range(T):
                    tok = slice(t * P, (t + 1) * P)
                    op = mm3(O[:, t // 2, (t % 2) * D:(t % 2 + 1) * D], h_hi[:, tok], h_lo[:, tok],
                             w2_s[0][:, f, :], w2_s[1][:, f, :], False, f == NF - 1)
                op.then_inc(S["f_o"], 1)

            def b_turn(b):
                pe.wait_ge(S["b_xn"], at(b, 1, 1))
                turn(Y, xn_b, S["b_xnT"])

            def b_kqv(b, t):
                dst = (Y, X)[t % 2]
                if t == 0:
                    pe.wait_ge(S["b_xT_hi"], at(b, 1, 1))
                    pe.wait_ge(S["b_xT_lo"], at(b, 1, 1))
                elif t == 1:
                    if not (b is NB - 1):
                        pe.wait_ge(S["a1_xT_lo"], at(b, 1, 2))
                    else:
                        pe.wait_ge(S["b3_xT_lo"], at(b, 1, 0))
                else:
                    pe.wait_ge(S["b_kqv_n"], at(b, T, t - 1))
                tok = slice(t * P, (t + 1) * P)
                for bank, col, width in ((0, 0, 2 * D), (1, 2 * D, D)):
                    cols = slice(col, col + width)
                    pe.matmul(dst[:, bank, 0:width], ones_b[:], bkqv_rows[:, cols], start=True, stop=False,
                              skip_group_check=True)
                    for k in range(C):
                        op = mm3(dst[:, bank, 0:width], xT_s[0][:, k, tok], xT_s[1][:, k, tok],
                                 wkqv_s[0][:, k, cols], wkqv_s[1][:, k, cols], False, k == C - 1)
                op.then_inc(S["b_kqv"], 1)

            def b_kq_turn(b, which):
                dst, done = ((Y, S["b_kT"]), (X, S["b_qT"]))[which]
                pe.wait_ge(S["b_kqv_n"], at(b, T, T))
                turn(dst, kq_n[:, :, which * D:(which + 1) * D], done)

            def b_scores(b, pair):
                dst = (Y, X)[pair]
                if pair == 0:
                    pe.wait_ge(S["b_kT_lo"], at(b, 1, 1))
                    pe.wait_ge(S["b_qT_lo"], at(b, 1, 1))
                for t in range(2):
                    tok = slice((2 * pair + t) * P, (2 * pair + t + 1) * P)
                    for c in range(C):
                        op = mm3(dst[:, t, :], kqT_s[0][:, c, tok], kqT_s[1][:, c, tok],
                                 kqT_s[0][:, C + c, :], kqT_s[1][:, C + c, :], c == 0, c == C - 1)
                op.then_inc(S["b_sc"], 1)

            def b_prob_turn(b, pair):
                dst = (Y, X)[pair]
                pe.wait_ge(S["b_prob"], at(b, T, T))
                for j in range(2):
                    keys = slice((2 * pair + j) * P, (2 * pair + j + 1) * P)
                    for t in range(T):
                        op = pe.transpose(dst[:, j, t * P:(t + 1) * P], kq_n[:, t, keys], ident[:])
                op.then_inc(S["b_pT"], 1)

            def b_out(b):
                pe.wait_ge(S["b_pT_lo"], at(b, 2, 2))
                pe.wait_ge(S["b_v_lo"], at(b, 1, 1))
                for t in range(T):
                    tok = slice(t * P, (t + 1) * P)
                    for j in range(T):
                        op = mm3(Y[:, t // 2, (t % 2) * D:(t % 2 + 1) * D], kqT_s[0][:, j, tok], kqT_s[1][:, j, tok],
                                 v_s[0][:, j, :, 0:P], v_s[1][:, j, :, 0:P], t % 2 == 0 and j == 0, j == T - 1)
                op.then_inc(S["b_out"], 1)

            def b3_turn(b):
                pe.wait_ge(S["b3_xn"], at(b, 1, 1))
                turn(X, xn_b, S["b3_xnT"])

            def phase_1(i, has_a, has_prev, r):
                f_h(r, 0, x1T_s)
                f_h(r, 1, x1T_s)
                if has_prev:
                    b_out(i - 1)
                if has_a:
                    a_turn(i + 1, has_prev)
                f_router(r, x1T_s)
                f_h(r, 2, x1T_s)
                f_router_turn(r)
                if has_a:
                    a_q(i + 1, has_prev)
                    a_kv(i + 1, 0)
                    a_kv(i + 1, 1)
                f_o(r, 0)
                f_h(r, 3, x1T_s)
                f_o(r, 1)
                if has_prev:
                    if has_a:
                        pe.wait_ge(S["a_v_lo"], at(i + 1, 2, 1))
                    b3_turn(i - 1)
                f_h(r, 4, x1T_s)
                f_o(r, 2)
                if has_a:
                    a_km(i + 1)
                f_h(r, 5, x1T_s)
                f_o(r, 3)
                if has_a:
                    a_att(i + 1, has_prev)
                f_h(r, 6, x1T_s)
                f_o(r, 4)
                f_h(r, 7, x1T_s)
                f_o(r, 5)
                f_o(r, 6)
                f_o(r, 7)

            def phase_2(i, has_a, has_prev, r):
                if has_prev:
                    pe.wait_ge(S["b3_xT_lo"], at(i, 1, 0))
                    f_h(r, 0, x3T_s)
                    f_h(r, 1, x3T_s)
                if has_a:
                    a_out(i + 1)
                if has_prev:
                    f_router(r, x3T_s)
                    f_h(r, 2, x3T_s)
                    f_router_turn(r)
                b_turn(i)
                if has_prev:
                    f_h(r, 3, x3T_s)
                    f_o(r, 0)
                if has_a:
                    a1_turn(i + 1)
                if has_prev:
                    f_o(r, 1)
                b_kqv(i, 0)
                b_kqv(i, 1)
                if has_prev:
                    f_h(r, 4, x3T_s)
                    f_o(r, 2)
                b_kqv(i, 2)
                b_kqv(i, 3)
                if has_prev:
                    f_h(r, 5, x3T_s)
                    f_o(r, 3)
                b_kq_turn(i, 0)
                b_kq_turn(i, 1)
                if has_prev:
                    f_h(r, 6, x3T_s)
                    f_o(r, 4)
                    f_h(r, 7, x3T_s)
                    f_o(r, 5)
                b_scores(i, 0)
                b_scores(i, 1)
                if has_prev:
                    f_o(r, 6)
                    f_o(r, 7)
                b_prob_turn(i, 0)
                b_prob_turn(i, 1)

            pe.wait_ge(S["pool_const"], NCONST)
            a_turn(0, False)
            pe.wait_ge(S["w_lo"], NWT)
            pe.wait_ge(S["bias_rows"], 15 * 16)
            a_q(0, False)
            a_kv(0, 0)
            a_kv(0, 1)
            a_km(0)
            a_att(0, False)
            a_out(0)
            a1_turn(0)
            pe.wait_ge(S["a1_xT_lo"], 1)
            phase_1(0, True, False, 0)
            phase_2(0, True, False, 0)
            with pe.Fori(1, NB - 1) as loop_i:
                i, run = turns(pe, loop_i)
                phase_1(i, True, True, run)
                phase_2(i, True, True, run + 1)
            phase_1(NB - 1, False, True, 2 * NB - 3)
            phase_2(NB - 1, False, True, 2 * NB - 2)
            b_out(NB - 1)
            b3_turn(NB - 1)
            pe.wait_ge(S["b3_xT_lo"], NB)
            r = 2 * NB - 1
            f_router(r, x3T_s)
            f_h(r, 0, x3T_s)
            f_router_turn(r)
            f_h(r, 1, x3T_s)
            for f in range(NF):
                if f + 2 < NF:
                    f_h(r, f + 2, x3T_s)
                f_o(r, f)

        def by_chunk(tiles):
            return tiles.rearrange("p t (c d) -> p t c d", c=C)

        @block.scalar
        def _(act):
            def take_hi(dst, src, ready, value, done):
                act.wait_ge(ready, value)
                act.activation(dst, src, ACT.Copy).then_inc(done, 1)

            def elu_parts(exp_dst, relu_dst, src, exp_done, relu_done):
                act.activation(exp_dst, src, ACT.Exp).then_inc(exp_done, 1)
                act.activation(relu_dst, src, ACT.Relu).then_inc(relu_done, 1)

            def a_q(b):
                act.wait_ge(S["a_q"], at(b, 1, 1))
                elu_parts(tmp[:], q_f[:], Y[:], S["a_q_exp"], S["a_q_relu"])

            def a_kv(b, pair):
                src = (X, Y)[pair]
                act.wait_ge(S["a_kv"], at(b, 2, pair + 1))
                if pair == 0:
                    act.wait_ge(S["a_q_f"], at(b, 1, 1))
                half = tmp[:, pair, :].rearrange("p (t d) -> p t d", t=2)
                tiles = slice(2 * pair, 2 * pair + 2)
                elu_parts(half, k_f[:, tiles, :], src[:, :, 0:D], S["a_kv_exp"], S["a_kv_relu"])
                act.activation(v_s[0][:, tiles, :, 0:P], by_chunk(src[:, :, D:2 * D]), ACT.Copy).then_inc(S["a_v_hi"], 1)

            def a_den(b):
                act.wait_ge(S["a_den"], at(b, 1, 1))
                for c in range(C):
                    act.activation(tmp[:, c, :], Y[:, c, :], ACT.Identity, bias=z_eps[:, 0:1]) \
                        .then_inc(S["a_den_eps"], 1)

            def f_logits_T(r):
                act.wait_ge(S["f_router"], at(r, 1, 1))
                act.activation(logits_T[:], O[:, 0, :], ACT.Copy).then_inc(S["f_logits_T"], 1)

            def f_gelu(r, f):
                act.wait_ge(S["f_h"], at(r, NF, f + 1))
                if not (r is 0 and f < 2):
                    act.wait_ge(S["f_h_lo"], at(r, NF, f - 1))
                if not (r is 0 and f < HR):
                    act.wait_ge(S["f_o"], at(r, NF, f + 1 - HR))
                act.activation(h_s[f % HR][0][:], H[f % 2][:], ACT.Gelu_apprx_tanh, bias=b1_sb[:, f:f + 1]) \
                    .then_inc(S["f_h_hi"], 1)
                act.activation(h_f[f % 2][:], H[f % 2][:], ACT.Gelu_apprx_tanh, bias=b1_sb[:, f:f + 1]) \
                    .then_inc(S["f_gelu"], 1)

            def f_exp(r):
                act.wait_ge(S["f_shift"], at(r, 1, 1))
                act.activation(top_p[:], top_p[:], ACT.Exp).then_inc(S["f_exp"], 1)

            def b_kq_gain(b, which, full):
                src = (Y, X)[which]
                dst = (tmp, q_f)[which] if full else kqT_s[0][:, C * which:C * which + C, :]
                act.wait_ge(S[("b_kT", "b_qT")[which]], at(b, 1, 1))
                for c in range(C):
                    g = 2 * C * which + c
                    act.activation(dst[:, c, :], src[:, c, :], ACT.Identity, bias=kq_gain_sb[:, g + C:g + C + 1],
                                   scale=kq_gain_sb[:, g:g + 1]) \
                        .then_inc(S[f"b_{'kq'[which]}T_{'f' if full else 'hi'}"], 1)

            def b_v_hi(b):
                act.wait_ge(S["b_v_f"], at(b, 1, 1))
                act.activation(v_s[0][:, :, :, 0:P], by_chunk(v_f[:]), ACT.Copy).then_inc(S["b_v_hi"], 1)

            def b_exp(b, t):
                src = (Y, X)[t // 2]
                act.wait_ge(S["b_max"], at(b, 2, t // 2 + 1))
                act.activation(kq_n[:, t, :], src[:, t % 2, :], ACT.Exp, bias=row_negmax[:, t:t + 1],
                               accum_out=row_sum[:, t:t + 1]).then_inc(S["b_prob"], 1)

            def phase_1(i, has_a, has_prev, r):
                f_gelu(r, 0)
                f_gelu(r, 1)
                if has_a:
                    take_hi(xT_s[0][:], X[:], S["a_xnT"], at(i + 1, 1, 1), S["a_xT_hi"])
                f_logits_T(r)
                f_gelu(r, 2)
                if has_a:
                    a_q(i + 1)
                    a_kv(i + 1, 0)
                    a_kv(i + 1, 1)
                f_exp(r)
                f_gelu(r, 3)
                if has_prev:
                    take_hi(x3T_s[0][:], X[:], S["b3_xnT"], at(i, 1, 0), S["b3_xT_hi"])
                f_gelu(r, 4)
                f_gelu(r, 5)
                if has_a:
                    a_den(i + 1)
                f_gelu(r, 6)
                f_gelu(r, 7)

            def phase_2(i, has_a, has_prev, r):
                if has_prev:
                    f_gelu(r, 0)
                    f_gelu(r, 1)
                    f_logits_T(r)
                    f_gelu(r, 2)
                take_hi(xT_s[0][:], Y[:], S["b_xnT"], at(i, 1, 1), S["b_xT_hi"])
                if has_prev:
                    f_gelu(r, 3)
                if has_a:
                    take_hi(x1T_s[0][:], X[:], S["a1_xnT"], at(i, 1, 2), S["a1_xT_hi"])
                if has_prev:
                    f_gelu(r, 4)
                    f_gelu(r, 5)
                b_kq_gain(i, 0, False)
                b_kq_gain(i, 1, False)
                b_kq_gain(i, 1, True)
                if has_prev:
                    f_gelu(r, 6)
                    f_gelu(r, 7)
                b_v_hi(i)
                for t in range(T):
                    b_exp(i, t)
                if has_prev:
                    f_exp(r)
                for pair in range(2):
                    take_hi(kqT_s[0][:, 2 * pair:2 * pair + 2, :], (Y, X)[pair][:], S["b_pT"], at(i, 2, pair + 1),
                            S["b_pT_hi"])

            act.wait_ge(S["small_in"], 3 * 16)
            act.wait_ge(S["pool_const"], NCONST)
            take_hi(xT_s[0][:], X[:], S["a_xnT"], 1, S["a_xT_hi"])
            for n, (src, dst, view) in enumerate(places):
                act.wait_ge(S["w_in"], 16 * NWT)
                act.activation(dst[0][:, :, :], view, ACT.Copy).then_inc(S["w_hi"], 1)
            a_q(0)
            a_kv(0, 0)
            a_kv(0, 1)
            a_den(0)
            take_hi(x1T_s[0][:], X[:], S["a1_xnT"], 1, S["a1_xT_hi"])
            phase_1(0, True, False, 0)
            phase_2(0, True, False, 0)
            with act.Fori(1, NB - 1) as loop_i:
                i, run = turns(act, loop_i)
                phase_1(i, True, True, run)
                phase_2(i, True, True, run + 1)
            phase_1(NB - 1, False, True, 2 * NB - 3)
            phase_2(NB - 1, False, True, 2 * NB - 2)
            take_hi(x3T_s[0][:], X[:], S["b3_xnT"], NB, S["b3_xT_hi"])
            f_logits_T(2 * NB - 1)
            f_gelu(2 * NB - 1, 0)
            f_exp(2 * NB - 1)
            for f in range(1, NF):
                f_gelu(2 * NB - 1, f)

        @block.vector
        def _(dve):

            dve_places = iter(range(SPARE))

            def carry():
                n = next(dve_places)
                dve.memset(spare_dve[:, n:n + 1], 0.0)

            def take_lo(dst, src, hi, ready, value, done):
                dve.wait_ge(ready, value)
                dve.tensor_tensor(dst, src, hi.bitcast(F32), ALU.subtract).then_inc(done, 1)

            def norm_stats(b, pre, src, st, mv):
                for t in range(T):
                    op = dve.bn_stats(st[:, t, :], src[:, t, :])
                op.then_inc(S[f"{pre}_stats"], 1)
                dve.wait_ge(S[f"{pre}_stats"], at(b, 1, 1))
                carry()
                for t in range(T):
                    op = dve.bn_aggr(mv[:, t, :], st[:, t, :])
                op.then_inc(S[f"{pre}_mv"], 1)

            def norm_apply(b, pre, src, dst, mv, rs):
                dve.wait_ge(S[f"{pre}_rstd"], at(b, 1, 1))
                for t in range(T):
                    op = dve.tensor_scalar(dst[:, t, :], src[:, t, :], mv[:, t, 0:1], rs[:, t:t + 1],
                                           ALU.subtract, ALU.mult)
                op.then_inc(S[f"{pre}_xn"], 1)

            def a_stats(b):
                dve.wait_ge(S["x_in"], at(b, 16, 16))
                norm_stats(b, "a", x_in, stA, mvA)

            def a_norm(b):
                if b is not 0:
                    dve.wait_ge(S["a1_xnT"], at(b, 1, 0))
                norm_apply(b, "a", x_in, xn_a, mvA, rsA)

            def elu(dst, exp, exp_done, relu_done, value, done):
                dve.wait_ge(relu_done, value)
                dve.wait_ge(exp_done, value)
                dve.scalar_tensor_tensor(dst, exp, 1.0, dst, ALU.min, ALU.add).then_inc(done, 1)

            def a_q(b):
                elu(q_f[:], tmp[:], S["a_q_exp"], S["a_q_relu"], at(b, 1, 1), S["a_q_f"])

            def split_f(dst, src, pre, value):
                dve.wait_ge(S[f"{pre[0]}"], value)
                dve.tensor_copy(dst[0], src).then_inc(S[f"{pre[1]}_hi"], 1)
                take_lo(dst[1], src, dst[0], S[f"{pre[1]}_hi"], value, S[f"{pre[1]}_lo"])

            def a_q_split(b):
                split_f([q[:] for q in qT_s], q_f[:], ("a_q_f", "a_q"), at(b, 1, 1))

            def a_k(b, pair):
                tiles = slice(2 * pair, 2 * pair + 2)
                half = tmp[:, pair, :].rearrange("p (t d) -> p t d", t=2)
                elu(k_f[:, tiles, :], half, S["a_kv_exp"], S["a_kv_relu"], at(b, 2, pair + 1), S["a_k_f"])
                split_f([k[:, tiles, :] for k in k_s], k_f[:, tiles, :], ("a_k_f", "a_k"), at(b, 2, pair + 1))

            def a_v(b, pair):
                tiles = slice(2 * pair, 2 * pair + 2)
                take_lo(v_s[1][:, tiles, :, 0:P], by_chunk((X, Y)[pair][:, :, D:2 * D]), v_s[0][:, tiles, :, 0:P],
                        S["a_v_hi"], at(b, 2, pair + 1), S["a_v_lo"])

            def a_km(b):
                dve.wait_ge(S["a_km"], at(b, 1, 1))
                for c in range(C):
                    dve.tensor_tensor(km_f[:, c, :], Y[:, c, 0:P], head_mask[:], ALU.mult)
                for c in range(C):
                    op = dve.tensor_scalar(km_f[:, C + c, :], head_mask[:], Y[:, c, P:P + 1], None, ALU.mult)
                op.then_inc(S["a_km_f"], 1)
                split_f([km[:] for km in km_s], km_f[:], ("a_km_f", "a_km"), at(b, 1, 1))

            def a_z(b, c):
                dve.wait_ge(S["a_den_eps"], at(b, C, c + 1))
                dve.reciprocal(tmp[:, c, :], tmp[:, c, :]).then_inc(S["a_z"], 1)

            def a_attn(b):
                dve.wait_ge(S["a_z"], at(b, C, C))
                dve.wait_ge(S["a_att"], at(b, 1, 1))
                dve.tensor_tensor(q_f[:], X[:], tmp[:], ALU.mult).then_inc(S["a_attn"], 1)
                split_f([xT[:] for xT in xT_s], q_f[:], ("a_attn", "a_attn"), at(b, 1, 1))

            def a_x1(b):
                dve.wait_ge(S["a_out"], at(b, 1, 1))
                if b is not 0:
                    dve.wait_ge(S["f_y"], at(b, 2, -2) if b is not 1 else 1)
                dve.tensor_tensor(x1[:].rearrange("p (a t) d -> p a (t d)", a=2), X[:],
                                  x_in[:].rearrange("p (a t) d -> p a (t d)", a=2), ALU.add).then_inc(S["a_x1"], 1)
                dve.wait_ge(S["a_x1"], at(b, 1, 1))
                norm_stats(b, "a1", x1, stA, mvA)

            def a1_norm(b):
                norm_apply(b, "a1", x1, xn_a, mvA, rsA)

            def f_top(r):
                rows = O[:, 1, :].rearrange("p (t n) -> p t n", t=T)
                dve.wait_ge(S["f_router_turn"], at(r, 1, 1))
                dve.tensor_copy(logit_hi[:], rows[:, :, 0:E]).then_inc(S["f_logit_hi"], 1)
                dve.wait_ge(S["f_logit_hi"], at(r, 1, 1))
                dve.tensor_tensor(logits[:], rows[:, :, E:2 * E], logit_hi[:], ALU.add).then_inc(S["f_logits"], 1)
                dve.wait_ge(S["f_logits"], at(r, 1, 1))
                carry()
                for t in range(T):
                    op = dve.max(top[:, t, :], logits[:, t, :])
                op.then_inc(S["f_top"], 1)
                dve.wait_ge(S["f_top"], at(r, 1, 1))
                dve.tensor_tensor(top_p[:], top[:], top[:, :, 0:1].to_broadcast([P, T, E]), ALU.subtract) \
                    .then_inc(S["f_shift"], 1)

            def f_comb(r):
                dve.wait_ge(S["f_exp"], at(r, 1, 1))
                dve.tensor_reduce(p_sum[:], top_p[:], X_AXIS, ALU.add).then_inc(S["f_psum"], 1)
                dve.wait_ge(S["f_psum"], at(r, 1, 1))
                dve.reciprocal(p_rec[:], p_sum[:]).then_inc(S["f_prec"], 1)
                dve.wait_ge(S["f_prec"], at(r, 1, 1))
                dve.tensor_tensor(p2[:], top_p[:, :, 0:2], p_rec[:].unsqueeze(2).to_broadcast([P, T, 2]), ALU.mult) \
                    .then_inc(S["f_p2"], 1)
                dve.wait_ge(S["f_p2"], at(r, 1, 1))
                dve.tensor_tensor(t_sum[:], p2[:, :, 0], p2[:, :, 1], ALU.add).then_inc(S["f_tsum"], 1)
                dve.wait_ge(S["f_tsum"], at(r, 1, 1))
                dve.reciprocal(t_rec[:], t_sum[:]).then_inc(S["f_trec"], 1)
                dve.wait_ge(S["f_trec"], at(r, 1, 1))
                dve.tensor_tensor(p2[:], p2[:], t_rec[:].unsqueeze(2).to_broadcast([P, T, 2]), ALU.mult) \
                    .then_inc(S["f_comb_p"], 1)
                dve.wait_ge(S["f_comb_p"], at(r, 1, 1))
                dve.tensor_tensor(comb[:], p2[:, :, 0], p2[:, :, 1], ALU.add).then_inc(S["f_comb"], 1)

            def f_lo(r, f):
                if not (r is 0 and f < HR):
                    dve.wait_ge(S["f_o"], at(r, NF, f + 1 - HR))
                take_lo(h_s[f % HR][1][:], h_f[f % 2][:], h_s[f % HR][0][:], S["f_gelu"], at(r, NF, f + 1), S["f_h_lo"])

            def f_y(r, res, dst):
                dve.wait_ge(S["f_comb"], at(r, 1, 1))
                dve.wait_ge(S["f_o"], at(r, NF, NF))
                for t in range(T):
                    op = dve.scalar_tensor_tensor(dst[:, t, :], O[:, t // 2, (t % 2) * D:(t % 2 + 1) * D],
                                                  comb[:, t:t + 1], res[:, t, :], ALU.mult, ALU.add)
                op.then_inc(S["f_y"], 1)

            def b_norm(b, has_prev):
                dve.wait_ge(S["f_y"], at(b, 2, 0) if has_prev else 1)
                if has_prev:
                    dve.wait_ge(S["b3_xnT"], at(b, 1, 0))
                norm_stats(b, "b", x2, stF, mvF)

            def b_norm_apply(b):
                norm_apply(b, "b", x2, xn_b, mvF, rsF)

            def b_kqv(b, t):
                src = (Y, X)[t % 2]
                parts = (src[:, 0, 0:D], src[:, 0, D:2 * D], src[:, 1, 0:D])
                dve.wait_ge(S["b_kqv"], at(b, T, t + 1))
                for n in range(3):
                    op = dve.bn_stats(stK[:, t, n, :], parts[n])
                op.then_inc(S["b_kqv_stats"], 1)
                dve.wait_ge(S["b_kqv_stats"], at(b, T, t + 1))
                carry()
                for n in range(3):
                    op = dve.bn_aggr(mvK[:, t, n, :], stK[:, t, n, :])
                op.then_inc(S["b_kqv_mv"], 1)

            def b_kqv_n(b, t):
                src = (Y, X)[t % 2]
                dsts = (kq_n[:, t, 0:D], kq_n[:, t, D:2 * D], v_f[:, t, :])
                parts = (src[:, 0, 0:D], src[:, 0, D:2 * D], src[:, 1, 0:D])
                dve.wait_ge(S["b_kqv_rstd"], at(b, T, t + 1))
                for n in range(3):
                    op = dve.tensor_scalar(dsts[n], parts[n], mvK[:, t, n, 0:1], rsK[:, t, n:n + 1],
                                           ALU.subtract, ALU.mult)
                op.then_inc(S["b_kqv_n"], 1)

            def b_k_gain(b):
                dve.wait_ge(S["b_kT"], at(b, 1, 1))
                dve.wait_ge(S["b_kT_hi"], at(b, C, C))
                for c in range(C):
                    op = dve.tensor_scalar(tmp[:, c, :], Y[:, c, :], kq_gain_sb[:, c:c + 1],
                                           kq_gain_sb[:, C + c:C + c + 1], ALU.mult, ALU.add)
                op.then_inc(S["b_kT_f"], 1)

            def b_kq_lo(b, which):
                src = (tmp, q_f)[which]
                n = "kq"[which]
                dve.wait_ge(S[f"b_{n}T_hi"], at(b, C, C))
                take_lo(kqT_s[1][:, C * which:C * which + C, :], src[:], kqT_s[0][:, C * which:C * which + C, :],
                        S[f"b_{n}T_f"], at(b, C, C) if which else at(b, 1, 1), S[f"b_{n}T_lo"])

            def b_v_lo(b):
                take_lo(v_s[1][:, :, :, 0:P], by_chunk(v_f[:]), v_s[0][:, :, :, 0:P], S["b_v_hi"], at(b, 1, 1),
                        S["b_v_lo"])

            def b_max(b, pair):
                dve.wait_ge(S["b_sc"], at(b, 2, pair + 1))
                dve.tensor_reduce(row_negmax[:, 2 * pair:2 * pair + 2], (Y, X)[pair][:], X_AXIS, ALU.max,
                                  negate=True).then_inc(S["b_max"], 1)

            def b_pT_lo(b, pair):
                js = slice(2 * pair, 2 * pair + 2)
                take_lo(kqT_s[1][:, js, :], (Y, X)[pair][:], kqT_s[0][:, js, :], S["b_pT_hi"], at(b, 2, pair + 1),
                        S["b_pT_lo"])

            def b_x3(b):
                dve.wait_ge(S["b_prob"], at(b, T, T))
                dve.reciprocal(row_rec[:], row_sum[:]).then_inc(S["b_rec"], 1)
                dve.wait_ge(S["b_rec"], at(b, 1, 1))
                dve.wait_ge(S["b_res"], at(b, 1, 1))
                if not (b is 0):
                    dve.wait_ge(S["x_out"], at(b, 16, 16))
                dve.wait_ge(S["b_out"], at(b, 1, 1))
                for t in range(T):
                    op = dve.scalar_tensor_tensor(x3[:, t, :], Y[:, t // 2, (t % 2) * D:(t % 2 + 1) * D],
                                                  row_rec[:, t:t + 1], x2[:, t, :], ALU.mult, ALU.add)
                op.then_inc(S["b_x3"], 1)

            def b3_stats(b):
                dve.wait_ge(S["b_x3"], at(b, 1, 1))
                norm_stats(b, "b3", x3, stF, mvF)

            def b3_norm(b):
                norm_apply(b, "b3", x3, xn_b, mvF, rsF)

            def xT_lo(dst, src, hi, pre, b):
                take_lo(dst[:], src[:], hi[:], S[f"{pre}_xT_hi"], at(b, 1, 1), S[f"{pre}_xT_lo"])

            def phase_1(i, has_a, has_prev, r):
                if has_a:
                    a_stats(i + 1)
                f_lo(r, 0)
                if has_a:
                    a_norm(i + 1)
                f_lo(r, 1)
                if has_prev:
                    b_x3(i - 1)
                if has_a:
                    xT_lo(xT_s[1], X, xT_s[0], "a", i + 1)
                if has_prev:
                    b3_stats(i - 1)
                f_top(r)
                f_lo(r, 2)
                if has_prev:
                    b3_norm(i - 1)
                if has_a:
                    a_q(i + 1)
                    a_q_split(i + 1)
                    a_k(i + 1, 0)
                    a_v(i + 1, 0)
                    a_k(i + 1, 1)
                    a_v(i + 1, 1)
                f_lo(r, 3)
                f_comb(r)
                if has_prev:
                    xT_lo(x3T_s[1], X, x3T_s[0], "b3", i - 1)
                f_lo(r, 4)
                if has_a:
                    a_km(i + 1)
                f_lo(r, 5)
                if has_a:
                    a_z(i + 1, 0)
                f_lo(r, 6)
                if has_a:
                    a_z(i + 1, 1)
                f_lo(r, 7)
                if has_a:
                    a_attn(i + 1)
                f_y(r, x1, x2)
                b_norm(i, has_prev)

            def phase_2(i, has_a, has_prev, r):
                if has_prev:
                    f_lo(r, 0)
                b_norm_apply(i)
                if has_prev:
                    f_lo(r, 1)
                if has_a:
                    a_x1(i + 1)
                if has_prev:
                    f_top(r)
                if has_a:
                    a1_norm(i + 1)
                if has_prev:
                    f_lo(r, 2)
                xT_lo(xT_s[1], Y, xT_s[0], "b", i)
                if has_prev:
                    f_lo(r, 3)
                if has_a:
                    xT_lo(x1T_s[1], X, x1T_s[0], "a1", i + 1)
                b_kqv(i, 0)
                b_kqv(i, 1)
                b_kqv_n(i, 0)
                b_kqv_n(i, 1)
                if has_prev:
                    f_lo(r, 4)
                b_kqv(i, 2)
                b_kqv(i, 3)
                b_kqv_n(i, 2)
                b_kqv_n(i, 3)
                if has_prev:
                    f_lo(r, 5)
                b_k_gain(i)
                b_kq_lo(i, 0)
                b_kq_lo(i, 1)
                if has_prev:
                    f_lo(r, 6)
                    f_lo(r, 7)
                b_max(i, 0)
                b_max(i, 1)
                b_v_lo(i)
                if has_prev:
                    f_comb(r)
                    f_y(r, x3, x3)
                b_pT_lo(i, 0)
                b_pT_lo(i, 1)

            dve.wait_ge(S["bias_in"], 3 * 16)
            dve.tensor_copy(bias_b[0:1, 0, :], bias_f[:]).then_inc(S["bias_part"], 1)
            for n in range(1, 3):
                dve.wait_ge(S["bias_part"], 2 * n - 1)
                dve.tensor_tensor(bias_f[:], bias_f[:], bias_b[0:1, n - 1, :], ALU.subtract) \
                    .then_inc(S["bias_part"], 1)
                dve.wait_ge(S["bias_part"], 2 * n)
                dve.tensor_copy(bias_b[0:1, n, :], bias_f[:]).then_inc(S["bias_part"], 1)
            dve.memset(z_eps[:], 1e-6).then_inc(S["bias_part"], 1)
            a_stats(0)
            a_norm(0)
            xT_lo(xT_s[1], X, xT_s[0], "a", 0)
            for n, (src, dst, view) in enumerate(places):
                take_lo(dst[1][:, :, :], view, dst[0][:, :, :], S["w_hi"], n + 1, S["w_lo"])
            a_q(0)
            a_q_split(0)
            for pair in range(2):
                a_k(0, pair)
                a_v(0, pair)
            a_km(0)
            a_z(0, 0)
            a_z(0, 1)
            a_attn(0)
            a_x1(0)
            a1_norm(0)
            xT_lo(x1T_s[1], X, x1T_s[0], "a1", 0)
            phase_1(0, True, False, 0)
            phase_2(0, True, False, 0)
            with dve.Fori(1, NB - 1) as loop_i:
                i, run = turns(dve, loop_i)
                phase_1(i, True, True, run)
                phase_2(i, True, True, run + 1)
            phase_1(NB - 1, False, True, 2 * NB - 3)
            phase_2(NB - 1, False, True, 2 * NB - 2)
            b_x3(NB - 1)
            b3_stats(NB - 1)
            b3_norm(NB - 1)
            xT_lo(x3T_s[1], X, x3T_s[0], "b3", NB - 1)
            r = 2 * NB - 1
            f_top(r)
            f_lo(r, 0)
            f_lo(r, 1)
            f_comb(r)
            for f in range(2, NF):
                f_lo(r, f)
            f_y(r, x3, x3)

        @block.gpsimd
        def _(pool):

            pool_places = iter(range(SPARE))

            def carry():
                n = next(pool_places)
                pool.tensor_tensor(spare_pool[:, n:n + 1], neg_half[:, 0:1], neg_half[:, 0:1], ALU.mult)

            def rstd(dst, ve, mv, pre, count, width):
                pool.wait_ge(S[f"{pre}_mv"], count)
                carry()
                pool.tensor_scalar(ve, mv, EPS, None, ALU.add).then_inc(S[f"{pre}_ve"], 1)
                pool.wait_ge(S[f"{pre}_ve"], count)
                pool.tensor_tensor(dst, ve, neg_half[:, 0:width], ALU.pow).then_inc(S[f"{pre}_rstd"], 1)

            def norm_rstd(b, pre, ve, mv, rs):
                rstd(rs[:], ve[:], mv[:, :, 1], pre, at(b, 1, 1), T)

            def b_res(b):
                pool.wait_ge(S["b_xn"], at(b, 1, 1))
                pool.tensor_tensor(x2[:], x2[:], xn_b[:], ALU.add).then_inc(S["b_res"], 1)

            def b_kqv_rstd(b, t):
                rstd(rsK[:, t, :], veK[:, t, :], mvK[:, t, :, 1], "b_kqv", at(b, T, t + 1), 3)

            def b_v(b):
                pool.wait_ge(S["b_kqv_n"], at(b, T, T))
                pool.tensor_tensor(v_f[:], v_f[:], v_gain_sb[:].unsqueeze(1).to_broadcast([P, T, D]), ALU.mult) \
                    .then_inc(S["b_v_g"], 1)
                pool.wait_ge(S["b_v_g"], at(b, 1, 1))
                pool.tensor_tensor(v_f[:], v_f[:], v_beta_sb[:].unsqueeze(1).to_broadcast([P, T, D]), ALU.add) \
                    .then_inc(S["b_v_f"], 1)

            def phase_1(i, has_a, has_prev, r):
                if has_a:
                    norm_rstd(i + 1, "a", veA, mvA, rsA)
                if has_prev:
                    norm_rstd(i - 1, "b3", veF, mvF, rsF)
                norm_rstd(i, "b", veF, mvF, rsF)

            def phase_2(i, has_a, has_prev, r):
                if has_a:
                    norm_rstd(i + 1, "a1", veA, mvA, rsA)
                b_res(i)
                for t in range(T):
                    b_kqv_rstd(i, t)
                b_v(i)

            done = 0

            def const(op):
                nonlocal done
                op.then_inc(S["pool_const"], 1)
                done += 1
                pool.wait_ge(S["pool_const"], done)

            for rows in (bout_rows, b2_rows, bkqv_rows):
                pool.memset(rows[:], 0.0).then_inc(S["zeroed"], 1)
            const(pool.memset(ident[:], 0.0))
            const(pool.affine_select(out=ident[:], in_=ident[:], compare_op=ALU.not_equal, fill=1.0, base=0,
                                     pattern=[[-1, P]], channel_multiplier=1))
            const(pool.memset(head_mask[:], 1.0))
            by_head = head_mask[:].rearrange("p (h d) -> p h d", d=HD)
            const(pool.affine_select(out=by_head, in_=by_head, compare_op=ALU.is_ge, fill=0.0, base=0,
                                     pattern=[[-HD, P // HD], [0, HD]], channel_multiplier=1))
            const(pool.affine_select(out=by_head, in_=by_head, compare_op=ALU.is_ge, fill=0.0, base=HD - 1,
                                     pattern=[[HD, P // HD], [0, HD]], channel_multiplier=-1))
            const(pool.memset(wr_s[:].bitcast(F32), 0.0))
            for part in range(2):
                const(pool.memset(v_s[part][:, :, :, P:VW].bitcast(F32), 1.0 - part))
            const(pool.memset(ones_b[:], 1.0))
            const(pool.memset(neg_half[:], -0.5))

            pool.wait_ge(S["small_in"], 3 * 16)
            pool.wait_ge(S["x_out"], 16)
            norm_rstd(0, "a", veA, mvA, rsA)
            norm_rstd(0, "a1", veA, mvA, rsA)
            phase_1(0, True, False, 0)
            phase_2(0, True, False, 0)
            with pool.Fori(1, NB - 1) as loop_i:
                i, run = turns(pool, loop_i)
                phase_1(i, True, True, run)
                phase_2(i, True, True, run + 1)
            phase_1(NB - 1, False, True, 2 * NB - 3)
            phase_2(NB - 1, False, True, 2 * NB - 2)
            norm_rstd(NB - 1, "b3", veF, mvF, rsF)


def kernel(**inputs):
    import numpy as np
    import concourse.bacc as bacc
    from concourse.bass_utils import run_bass_kernel_spmd

    g = {name: np.asarray(a) for name, a in inputs.items()}

    def cols(v):
        return v.reshape(-1, P).T

    b = "L0_attn_b_"
    arrays = {
        "x": g["L0_attn_a_x"],
        "w_qkv": g["L0_attn_a_w_qkv"].T,
        "w_out": g["L0_attn_a_w_out"].T,
        "b_out": g["L0_attn_a_b_out"].reshape(1, -1),
        "w_kqv": np.concatenate([g[b + "Wk"], g[b + "Wq"], g[b + "Wv"]], axis=1),
        "b_kqv": np.concatenate([g[b + "bk"], g[b + "bq"], g[b + "bv"]]).reshape(1, -1),
        "kq_gain": np.concatenate([cols(g[b + n]) for n in ("gk", "betak", "gq", "betaq")], axis=1),
        "v_gain": g[b + "gv"],
        "v_beta": g[b + "betav"],
        "router_w": g["L0_ffn_router_w"],
        "w1": g["L0_ffn_w1"],
        "b1": cols(g["L0_ffn_b1"]),
        "w2": g["L0_ffn_w2"],
        "b2": g["L0_ffn_b2"].reshape(1, -1),
    }
    arrays = {name: np.ascontiguousarray(a) for name, a in arrays.items()}
    nc = bacc.Bacc("TRN2", target_bir_lowering=False, num_devices=1)
    args = [nc.dram_tensor(name, a.shape, mybir.dt.from_np(a.dtype), kind="ExternalInput").ap()
            for name, a in arrays.items()]
    out = nc.dram_tensor("out", arrays["x"].shape, F32, kind="ExternalOutput").ap()
    hybrid_block(nc, *args, out)
    r = run_bass_kernel_spmd(nc, [arrays], core_ids=[0])
    return r.results[0]["out"]
```

```python
from contextlib import ExitStack

import concourse.bass as bass
from concourse import mybir

F32 = mybir.dt.float32
F32R = mybir.dt.float32r
BF16 = mybir.dt.bfloat16
ALU = mybir.AluOpType
ACT = mybir.ActivationFunctionType
X_AXIS = mybir.AxisListType.X

P = 128
PARTS = ("hi", "lo")


class Turn:

    def __init__(self, multiples, scale, offset):
        self.multiples, self.scale, self.offset = multiples, scale, offset

    def __add__(self, n):
        return Turn(self.multiples, self.scale, self.offset + n)

    def __sub__(self, n):
        return self + -n

    def times(self, n):
        return Turn(self.multiples, self.scale * n, self.offset * n)


def turns(eng, i):
    multiples = {m: eng.snap(i * m) for m in (1, 2, 4, 8, 16)}
    batch = Turn(multiples, 1, 0)
    return batch, batch.times(2) - 1


def at(turn, per_turn, k):
    if isinstance(turn, Turn):
        count = turn.offset * per_turn + k
        value = turn.multiples[turn.scale * per_turn]
        return value + count if count else value
    return turn * per_turn + k


def hybrid_block(nc, x, w_qkv, w_out, b_out, w_kqv, b_kqv, kq_gain, v_gain, v_beta,
                 router_w, w1, b1, w2, b2, out):
    NB, N, D = x.shape
    T = N // P
    C = D // P
    FF = w1.shape[1]
    NF = FF // P
    E = router_w.shape[1]
    HD = 16
    EPS = 1e-5
    assert (T, C, N, E) == (4, 2, 512, 8) and NF == 8

    def tiles_of(half):
        return range(T) if half is None else range(half * (T // 2), (half + 1) * (T // 2))

    with ExitStack() as ctx:
        def sb(name, shape, dt=F32, cx=ctx):
            return cx.enter_context(nc.sbuf_tensor(name, shape, dt))

        def split(name, shape):
            return [sb(f"{name}_{part}", shape, F32R) for part in PARTS]

        def sem(name):
            return ctx.enter_context(nc.semaphore(name))

        wqkv_s = split("wqkv", [P, C, 3 * D])
        wout_s = split("wout", [P, C, D])
        wkqv_s = split("wkqv", [P, C, 3 * D])
        wr_s = sb("wr", [P, C, P], F32R)
        w1_s = split("w1", [P, C, FF])
        w2_s = split("w2", [P, NF, D])
        ident = sb("ident", [P, P])
        head_mask = sb("head_mask", [P, P])
        ones_b = sb("ones_b", [P, P], BF16)
        bkqv_rows = sb("bkqv_rows", [P, 3 * D], BF16)
        bout_sb = sb("bout_sb", [P, D])
        b2_sb = sb("b2_sb", [P, D])
        b2_comb = sb("b2_comb", [P, T, D])
        kq_gain_sb = sb("kq_gain_sb", [P, 4 * C])
        b1_sb = sb("b1_sb", [P, NF])
        v_gain_sb = sb("v_gain_sb", [P, D])
        v_beta_sb = sb("v_beta_sb", [P, D])
        neg_half = sb("neg_half", [P, 3 * T])
        z_eps = sb("z_eps", [P, 1])
        SPARE = 256
        spare_dve, spare_pool = sb("spare_dve", [P, SPARE], BF16), sb("spare_pool", [P, SPARE], BF16)
        stA, stF, stK = sb("stA", [P, T, 6]), sb("stF", [P, T, 6]), sb("stK", [P, T, 3, 6])
        mvA, mvF, mvK = sb("mvA", [P, T, 2]), sb("mvF", [P, T, 2]), sb("mvK", [P, T, 3, 2])
        rsA, rsF, rsK = sb("rsA", [P, T]), sb("rsF", [P, T]), sb("rsK", [P, T, 3])
        veA, veF, veK = sb("veA", [P, T]), sb("veF", [P, T]), sb("veK", [P, T, 3])
        logit_hi = sb("logit_hi", [P, T, E])
        logits = sb("logits", [P, T, E])
        top = sb("top", [P, T, E])
        top_p = sb("top_p", [P, T, E])
        p_sum, p_rec = sb("p_sum", [P, T]), sb("p_rec", [P, T])
        t_sum, t_rec = sb("t_sum", [P, T]), sb("t_rec", [P, T])
        comb = sb("comb", [P, T])
        p2 = sb("p2", [P, T, 2])
        row_negmax, row_sum, row_rec = sb("row_negmax", [P, T]), sb("row_sum", [P, T]), sb("row_rec", [P, T])
        x_in = sb("x_in", [P, T, D])
        xn_a = sb("xn_a", [P, T, D])
        xn_b = sb("xn_b", [P, T, D])
        xT_s = split("xT", [P, C, N])
        q_f = sb("q_f", [P, C, N])
        km_f = q_f[:, 0, :].rearrange("p (c n) -> p c n", c=2 * C)
        km_lo_f = q_f[:, 1, 0:C * P].rearrange("p (c n) -> p c n", c=C)
        logits_T = q_f[:, 1, :]
        tmp = sb("tmp", [P, C, N])
        qT_s = split("qT", [P, C, N])
        k_s = split("k", [P, T, D])
        VW = P + 2
        v_all = sb("v", [P, 2, T, C, VW], F32R)
        v_s = [v_all[:, part] for part in range(2)]
        v_f = sb("v_f", [P, T, D])
        km_s = split("km", [P, 2 * C, P])
        stage_cx = ExitStack()
        NW = C * 3 * D * 2 + C * D + C * E + C * FF + NF * D
        stage = sb("stage", [P, NW], F32, stage_cx)
        bias_f = sb("bias_f", [1, 3 * D], F32, stage_cx)
        bias_b = sb("bias_b", [1, 3, 3 * D], BF16, stage_cx)
        stage_cx.close()
        kq_n = sb("kq_n", [P, T, 2 * D])
        k_f = kq_n[:, :, 0:D]
        x1 = sb("x1", [P, T, D])
        x1T_s = split("x1T", [P, C, N])
        x2 = sb("x2", [P, T, D])
        kqT_s = split("kqT", [P, 2 * C, N])
        x3 = sb("x3", [P, T, D])
        x3T_s = split("x3T", [P, C, N])
        HR = 4
        h_f = [sb(f"h_f{n}", [P, N]) for n in range(2)]
        h_s = [split(f"h{n}", [P, N]) for n in range(HR)]

        X = ctx.enter_context(nc.psum_tensor("X", [P, 2, 512], F32))
        Y = ctx.enter_context(nc.psum_tensor("Y", [P, 2, 512], F32))
        O = ctx.enter_context(nc.psum_tensor("O", [P, 2, 512], F32))
        H = [ctx.enter_context(nc.psum_tensor(f"H{n}", [P, 512], F32)) for n in range(2)]

        names = """small_in bias_in bias_rows w_hi w_lo pool_const zeroed bias_part z_eps
        x_in x_out
        a_stats a_mv a_ve a_rstd a_xn a_xnT a_xT_hi a_xT_lo
        a_q a_q_exp a_q_relu a_q_f a_q_hi a_q_lo
        a_kv a_kv_exp a_kv_relu a_k_f a_k_hi a_k_lo a_v_hi a_v_lo
        a_km a_km_part a_km_f a_km_hi a_km_lo a_att a_den a_den_eps a_z a_attn a_attn_hi a_attn_lo
        a_res a_out a_x1 a1_stats a1_mv a1_ve a1_rstd a1_xn a1_xnT a1_xT_hi a1_xT_lo
        f_router f_logits_T f_router_turn f_logit_hi f_logits f_top f_shift f_exp f_psum f_prec f_p2 f_tsum f_trec f_comb_p f_comb f_b2 f_res
        f_h f_h_hi f_gelu f_h_lo f_o f_y f_y_tile
        half_out half_sum half_stats half_mv half_ve half_rstd half_xn half_xnT half_xT_hi half_xT_lo
        b_stats b_mv b_ve b_rstd b_xn b_res b_xnT b_xT_hi b_xT_lo
        b_kqv b_kqv_stats b_kqv_mv b_kqv_ve b_kqv_rstd b_kqv_n b_v_g b_v_f b_v_hi b_v_lo
        b_kq_n b_kT b_kT_f b_kT_hi b_kT_lo b_qT b_qT_f0 b_qT_f1 b_qT_hi b_qT_lo
        b_sc b_max b_prob b_pT b_pT_hi b_pT_lo b_rec b_out b_x3
        b3_stats b3_mv b3_ve b3_rstd b3_xn b3_xnT b3_xT_hi b3_xT_lo""".split()
        S = {n: sem(n) for n in names}
        A1_FIRST, B_FIRST, B3_LAST, F_LAST = range(4)

        def step(name, kind, b, half, place):
            return (S[f"half_{kind}"], place + 1) if half == 0 else (S[name], at(b, 1, 1))

        def norm_step(pre, kind, b, half, place):
            return step(f"{pre}_{kind}", kind, b, half, place)

        W_QKV, W_OUT, W_R, W_1, W_KQV, W_2 = range(6)
        w_in = [sem(f"w_in{n}") for n in range(6)]

        places, base = [], 0
        for src, dst in ((w_qkv, wqkv_s), (w_out, wout_s),
                         (router_w, [wr_s[:, :, 0:E], wr_s[:, :, E:2 * E]]), (w1, w1_s), (w_kqv, wkqv_s), (w2, w2_s)):
            chunks, width = src.shape[0] // P, src.shape[1]
            view = stage[:, base:base + chunks * width].rearrange("p (c n) -> p c n", c=chunks)
            places.append((src, dst, view))
            base += chunks * width
        NWT = len(places)
        NCONST = 10

        block = ctx.enter_context(nc.Block())

        def b_in(b):
            return x3T_s if b == 0 else xT_s

        @block.sync
        def _(sp):
            def load_x(b, peeled=False):
                if not (peeled and b == 0):
                    sp.wait_ge(S["a_x1"], at(b, 1, 0))
                sp.dma_start(x_in[:], x[bass.ds(b, 1)].rearrange("o (t p) d -> p (o t) d", p=P)) \
                    .then_inc(S["x_in"], 16)

            def store_out(b):
                sp.wait_ge(S["f_y"], 2 * b + 3)
                sp.dma_start(out[bass.ds(b, 1)].rearrange("o (t p) d -> p (o t) d", p=P), xn_b[:]) \
                    .then_inc(S["x_out"], 16)

            load_x(0, True)
            for n, (src, dst, view) in enumerate(places):
                sp.dma_start(view, src.rearrange("(c p) n -> p c n", p=P)).then_inc(w_in[n], 16)
                if n == W_OUT:
                    sp.dma_start(bias_f[:], b_kqv).then_inc(S["bias_in"], 16)
            sp.dma_start(kq_gain_sb[:], kq_gain).then_inc(S["small_in"], 16)
            sp.dma_start(b1_sb[:], b1).then_inc(S["small_in"], 16)
            sp.dma_start(bout_sb[:], b_out.partition_broadcast(P)).then_inc(S["small_in"], 16)
            sp.dma_start(b2_sb[:], b2.partition_broadcast(P)).then_inc(S["small_in"], 16)
            sp.dma_start(v_gain_sb[:], v_gain.partition_broadcast(P)).then_inc(S["small_in"], 16)
            sp.dma_start(v_beta_sb[:], v_beta.partition_broadcast(P)).then_inc(S["x_out"], 16)
            sp.wait_ge(S["bias_part"], 5)
            sp.wait_ge(S["zeroed"], 1)
            for row in range(3):
                sp.dma_start(bkqv_rows[row:row + 1, :], bias_b[0:1, row, :]).then_inc(S["bias_rows"], 16)
            load_x(1)
            load_x(2)
            with sp.Fori(1, NB - 2) as i:
                load_x(i + 2)
                store_out(i - 1)
            store_out(NB - 3)
            store_out(NB - 2)
            for t in range(T):
                sp.wait_ge(S["f_y_tile"], t + 1)
                sp.dma_start(out[NB - 1, t * P:(t + 1) * P, :], xn_b[:, t, :]).then_inc(S["x_out"], 16)
            sp.wait_ge(S["x_out"], 16 * (NB + T))

        @block.tensor
        def _(pe):
            def mm3(dst, l_hi, l_lo, r_hi, r_lo, start, stop):
                pe.matmul(dst, l_hi, r_hi, start=start, stop=False, skip_group_check=True)
                pe.matmul(dst, l_hi, r_lo, start=False, stop=False, skip_group_check=True)
                return pe.matmul(dst, l_lo, r_hi, start=False, stop=stop, skip_group_check=True)

            HI, LO = 0, 1
            HI_STATIONARY, LO_STATIONARY = ((HI, HI), (HI, LO)), ((LO, HI),)
            HI_MOVING, LO_MOVING = ((HI, HI), (LO, HI)), ((HI, LO),)

            def turn(dst, src, done):
                for c in range(C):
                    for t in range(T):
                        op = pe.transpose(dst[:, c, t * P:(t + 1) * P], src[:, t, c * P:(c + 1) * P], ident[:])
                op.then_inc(done, 1)

            def turn_half(pre, dst, src, b, half, place):
                pe.wait_ge(*norm_step(pre, "xn", b, half, place))
                for t in tiles_of(half):
                    for c in range(C):
                        op = pe.transpose(dst[:, c, t * P:(t + 1) * P], src[:, t, c * P:(c + 1) * P], ident[:])
                op.then_inc(norm_step(pre, "xnT", b, half, place)[0], 1)

            def a_turn(b, prev):
                pe.wait_ge(S["a_xn"], at(b, 1, 1))
                if prev:
                    pe.wait_ge(S["b_pT_lo"], at(b - 1, 2, 0))
                elif b != 0:
                    pe.wait_ge(S["a1_xT_lo"], at(b, 1, 0))
                turn(X, xn_a, S["a_xnT"])

            def a_q(b, prev):
                pe.wait_ge(S["a_xT_hi"], at(b, 1, 1))
                if prev:
                    pe.wait_ge(S["b_x3"], at(b - 1, 1, 0))
                for passes in (HI_MOVING, LO_MOVING):
                    if passes is LO_MOVING:
                        pe.wait_ge(S["a_xT_lo"], at(b, 1, 1))
                    for m in range(C):
                        for k in range(C):
                            for w, x in passes:
                                op = pe.matmul(Y[:, m, :], wqkv_s[w][:, k, m * P:(m + 1) * P], xT_s[x][:, k, :],
                                               start=(k == 0 and passes is HI_MOVING and w == HI),
                                               stop=(k == C - 1 and passes is LO_MOVING), skip_group_check=True)
                op.then_inc(S["a_q"], 1)

            def a_kv(b, pair):
                dst = (X, Y)[pair]
                if pair:
                    pe.wait_ge(S["a_q_relu"], at(b, 1, 1))
                for t in range(2):
                    tok = slice((2 * pair + t) * P, (2 * pair + t + 1) * P)
                    for k in range(C):
                        op = mm3(dst[:, t, :], xT_s[0][:, k, tok], xT_s[1][:, k, tok],
                                 wqkv_s[0][:, k, D:3 * D], wqkv_s[1][:, k, D:3 * D], k == 0, k == C - 1)
                op.then_inc(S["a_kv"], 1)

            def a_km(b):
                pe.wait_ge(S["a_k_lo"], at(b, 2, 2))
                pe.wait_ge(S["a_v_lo"], at(b, 2, 2))
                for c in range(C):
                    ch = slice(c * P, (c + 1) * P)
                    for t in range(T):
                        pe.matmul(Y[:, c, 0:2 * VW].rearrange("p (h n) -> p h n", h=2), k_s[0][:, t, ch],
                                  v_all[:, :, t, c, :], start=(t == 0), stop=False, skip_group_check=True)
                        op = pe.matmul(Y[:, c, 0:VW], k_s[1][:, t, ch], v_s[0][:, t, c, :], start=False,
                                       stop=(t == T - 1), skip_group_check=True)
                op.then_inc(S["a_km"], 1)

            def a_att(b, prev):
                pe.wait_ge(S["a_km_hi"], at(b, 1, 1))
                pe.wait_ge(S["a_q_lo"], at(b, 1, 1))
                if prev:
                    pe.wait_ge(S["b3_xT_lo"], at(b - 1, 1, 0))
                for dst, first, done in ((Y, C, "a_den"), (X, 0, "a_att")):
                    for passes in (HI_STATIONARY, LO_STATIONARY):
                        if dst is Y and passes is LO_STATIONARY:
                            pe.wait_ge(S["a_km_lo"], at(b, 1, 1))
                        for c in range(C):
                            for m, q in passes:
                                op = pe.matmul(dst[:, c, :], km_s[m][:, first + c, :], qT_s[q][:, c, :],
                                               start=(m == HI and q == HI), stop=(m == LO), skip_group_check=True)
                            if passes is LO_STATIONARY:
                                op.then_inc(S[done], 1)

            def a_out(b, halves=False):
                for passes, ready in ((HI_STATIONARY, "a_attn_hi"), (LO_STATIONARY, "a_attn_lo")):
                    for c in range(C):
                        pe.wait_ge(S[ready], at(b, C, c + 1))
                        if c == 0 and passes is HI_STATIONARY:
                            pe.wait_ge(S["a_attn"], at(b, C, C))
                        for t in range(T):
                            for a, w in passes:
                                op = pe.matmul(X[:, t // 2, (t % 2) * D:(t % 2 + 1) * D],
                                               xT_s[a][:, c, t * P:(t + 1) * P], wout_s[w][:, c, :],
                                               start=(c == 0 and a == HI and w == HI and t % 2 == 0),
                                               stop=(c == C - 1 and a == LO), skip_group_check=True)
                            if halves and c == C - 1 and passes is LO_STATIONARY and t == 1:
                                op.then_inc(S["half_out"], 1)
                op.then_inc(S["a_out"], 1)

            def a1_turn(b, dst):
                pe.wait_ge(S["a1_xn"], at(b, 1, 1))
                turn(dst, xn_a, S["a1_xnT"])

            def f_router(r, xs):
                if r != 0:
                    pe.wait_ge(S["f_y"], at(r, 1, 0))
                for c in range(C):
                    for part in range(2):
                        op = pe.matmul(O[:, 0, :], wr_s[:, c, :], xs[part][:, c, :], start=(c == 0 and part == 0),
                                       stop=(c == C - 1 and part == 1))
                op.then_inc(S["f_router"], 1)

            def f_router_turn(r):
                pe.wait_ge(S["f_logits_T"], at(r, 1, 1))
                for t in range(T):
                    op = pe.transpose(O[:, 1, t * P:(t + 1) * P], logits_T[:, t * P:(t + 1) * P], ident[:])
                op.then_inc(S["f_router_turn"], 1)

            def f_h(r, f, xs):
                if not (r == 0 and f < 2):
                    pe.wait_ge(S["f_gelu"], at(r, NF, f - 1))
                ch = slice(f * P, (f + 1) * P)
                for k in range(C):
                    op = mm3(H[f % 2][:], w1_s[0][:, k, ch], w1_s[1][:, k, ch], xs[0][:, k, :], xs[1][:, k, :],
                             k == 0, k == C - 1)
                op.then_inc(S["f_h"], 1)

            def f_o(r, f, halves=False):
                pe.wait_ge(S["f_h_hi"], at(r, NF, f + 1))
                if f == 0:
                    pe.wait_ge(S["f_logits"], at(r, 1, 1))
                for passes in (HI_STATIONARY, LO_STATIONARY):
                    if passes is LO_STATIONARY:
                        pe.wait_ge(S["f_h_lo"], at(r, NF, f + 1))
                    for t in range(T):
                        for h, w in passes:
                            op = pe.matmul(O[:, t // 2, (t % 2) * D:(t % 2 + 1) * D],
                                           h_s[f % HR][h][:, t * P:(t + 1) * P], w2_s[w][:, f, :],
                                           start=(f == 0 and h == HI and w == HI and t % 2 == 0),
                                           stop=(f == NF - 1 and h == LO), skip_group_check=True)
                        if halves and passes is LO_STATIONARY and t == 1:
                            op.then_inc(S["half_out"], 1)
                op.then_inc(S["f_o"], 1)

            def b_turn(b):
                pe.wait_ge(S["b_xn"], at(b, 1, 1))
                turn(Y, xn_b, S["b_xnT"])

            def b_kqv(b, t):
                dst = (Y, X)[t % 2]
                if t == 0:
                    pe.wait_ge(S["b_xT_hi"], at(b, 1, 1))
                    pe.wait_ge(S["b_xT_lo"], at(b, 1, 1))
                elif t == 1:
                    if b == 0:
                        pe.wait_ge(S["a_x1"], 2)
                    elif not (b == NB - 1):
                        pe.wait_ge(S["a1_xT_lo"], at(b, 1, 2))
                    else:
                        pe.wait_ge(S["b3_xT_lo"], at(b, 1, 0))
                tok = slice(t * P, (t + 1) * P)
                for bank, col, width in ((0, 0, 2 * D), (1, 2 * D, D)):
                    cols = slice(col, col + width)
                    if t >= 2:
                        pe.wait_ge(S[("b_kq_n", "b_kqv_n")[bank]], at(b, T, t - 1))
                    pe.matmul(dst[:, bank, 0:width], ones_b[:], bkqv_rows[:, cols], start=True, stop=False,
                              skip_group_check=True)
                    for k in range(C):
                        op = mm3(dst[:, bank, 0:width], b_in(b)[0][:, k, tok], b_in(b)[1][:, k, tok],
                                 wkqv_s[0][:, k, cols], wkqv_s[1][:, k, cols], False, k == C - 1)
                op.then_inc(S["b_kqv"], 1)

            def b_kq_turn(b, which):
                dst, done = ((Y, S["b_kT"]), (X, S["b_qT"]))[which]
                for t in range(T):
                    if which == 0 and t == 0:
                        pe.wait_ge(S["b_kqv_n"], at(b, T, 3))
                    elif which == 0 and t == T - 1:
                        pe.wait_ge(S["b_kq_n"], at(b, T, T))
                    elif which == 1 and t == 0:
                        pe.wait_ge(S["b_kqv_n"], at(b, T, T))
                    for c in range(C):
                        ch = slice((which * C + c) * P, (which * C + c + 1) * P)
                        op = pe.transpose(dst[:, c, t * P:(t + 1) * P], kq_n[:, t, ch], ident[:])
                op.then_inc(done, 1)

            def b_scores(b, pair):
                dst = (Y, X)[pair]
                if pair == 0:
                    pe.wait_ge(S["b_kT_hi"], at(b, C, C))
                    pe.wait_ge(S["b_qT_hi"], at(b, C, C))
                    pe.wait_ge(S["b_kT_f"], at(b, C, C))
                for k, q in ((HI, HI), (LO, HI), (HI, LO)):
                    if pair == 0 and k == LO:
                        pe.wait_ge(S["b_kT_lo"], at(b, 1, 1))
                    if pair == 0 and q == LO:
                        pe.wait_ge(S["b_qT_lo"], at(b, C, C))
                    for t in range(2):
                        for c in range(C):
                            op = pe.matmul(dst[:, t, :], kqT_s[k][:, c, (2 * pair + t) * P:(2 * pair + t + 1) * P],
                                           kqT_s[q][:, C + c, :], start=(k == HI and q == HI and c == 0),
                                           stop=(q == LO and c == C - 1), skip_group_check=True)
                op.then_inc(S["b_sc"], 1)

            def b_prob_turn(b, pair):
                dst = (Y, X)[pair]
                for t in range(T):
                    if pair == 0 and t != 1:
                        pe.wait_ge(S["b_prob"], at(b, T, max(t + 1, 2)))
                    for j in range(2):
                        keys = slice((2 * pair + j) * P, (2 * pair + j + 1) * P)
                        op = pe.transpose(dst[:, j, t * P:(t + 1) * P], kq_n[:, t, keys], ident[:])
                op.then_inc(S["b_pT"], 1)

            def b_out(b, halves=False):
                pe.wait_ge(S["b_pT_hi"], at(b, 2, 2))
                pe.wait_ge(S["b_pT_lo"], at(b, 2, 1))
                pe.wait_ge(S["b_v_lo"], at(b, 1, 1))
                for passes in (HI_STATIONARY, LO_STATIONARY):
                    if passes is LO_STATIONARY:
                        pe.wait_ge(S["b_pT_lo"], at(b, 2, 2))
                    for t in range(T):
                        for j in range(T):
                            for p, v in passes:
                                op = pe.matmul(Y[:, t // 2, (t % 2) * D:(t % 2 + 1) * D],
                                               kqT_s[p][:, j, t * P:(t + 1) * P], v_s[v][:, j, :, 0:P],
                                               start=(p == HI and v == HI and t % 2 == 0 and j == 0),
                                               stop=(p == LO and j == T - 1), skip_group_check=True)
                        if halves and passes is LO_STATIONARY and t == 1:
                            op.then_inc(S["half_out"], 1)
                op.then_inc(S["b_out"], 1)

            def b3_turn(b):
                pe.wait_ge(S["b3_xn"], at(b, 1, 1))
                turn(X, xn_b, S["b3_xnT"])

            def keep_warm(n):
                for _ in range(n):
                    pe.matmul(H[1][:].rearrange("p (a n) -> p a n", n=P), ones_b[:],
                              ones_b[:].unsqueeze(1).to_broadcast([P, N // P, P]), start=True, stop=True)

            def phase_1(i, has_a, has_prev, r):
                f_h(r, 0, x1T_s)
                f_h(r, 1, x1T_s)
                if has_prev:
                    b_out(i - 1)
                f_router(r, x1T_s)
                f_h(r, 2, x1T_s)
                if has_a:
                    a_turn(i + 1, has_prev)
                f_router_turn(r)
                f_h(r, 3, x1T_s)
                if has_a:
                    a_q(i + 1, has_prev)
                    a_kv(i + 1, 0)
                    a_kv(i + 1, 1)
                f_o(r, 0)
                f_o(r, 1)
                if has_prev:
                    if has_a:
                        pe.wait_ge(S["a_v_lo"], at(i + 1, 2, 1))
                    b3_turn(i - 1)
                f_h(r, 4, x1T_s)
                f_o(r, 2)
                if has_a:
                    a_km(i + 1)
                f_h(r, 5, x1T_s)
                f_o(r, 3)
                if has_a:
                    a_att(i + 1, has_prev)
                f_h(r, 6, x1T_s)
                f_o(r, 4)
                f_h(r, 7, x1T_s)
                f_o(r, 5)
                f_o(r, 6)
                f_o(r, 7, i == 0)

            def phase_2(i, has_a, has_prev, r):
                if i == 0:
                    pe.wait_ge(S["f_gelu"], NF)
                    keep_warm(20)
                    turn_half("b", Y, xn_b, i, 0, B_FIRST)
                    turn_half("b", O, xn_b, i, 1, B_FIRST)
                    a_out(i + 1)
                else:
                    pe.wait_ge(S["b3_xT_lo"], at(i, 1, 0))
                    f_h(r, 0, x3T_s)
                    f_h(r, 1, x3T_s)
                    if has_a:
                        a_out(i + 1)
                    f_router(r, x3T_s)
                    f_h(r, 2, x3T_s)
                    f_router_turn(r)
                    f_h(r, 3, x3T_s)
                    b_turn(i)
                    f_o(r, 0)
                    f_o(r, 1)
                    f_h(r, 4, x3T_s)
                    if has_a:
                        a1_turn(i + 1, X)
                b_kqv(i, 0)
                b_kqv(i, 1)
                if has_prev:
                    f_o(r, 2)
                    f_h(r, 5, x3T_s)
                else:
                    keep_warm(10)
                b_kqv(i, 2)
                b_kqv(i, 3)
                if has_prev:
                    f_o(r, 3)
                    f_h(r, 6, x3T_s)
                    f_o(r, 4)
                else:
                    keep_warm(13)
                b_kq_turn(i, 0)
                b_kq_turn(i, 1)
                if has_prev:
                    f_h(r, 7, x3T_s)
                    f_o(r, 5)
                else:
                    keep_warm(10)
                b_scores(i, 0)
                b_scores(i, 1)
                if i == 0:
                    a1_turn(i + 1, O)
                if has_prev:
                    f_o(r, 6)
                    f_o(r, 7)
                b_prob_turn(i, 0)
                b_prob_turn(i, 1)

            pe.wait_ge(S["pool_const"], 2)
            keep_warm(20)
            pe.wait_ge(S["pool_const"], 4)
            a_turn(0, False)
            pe.wait_ge(S["w_lo"], W_QKV + 1)
            a_q(0, False)
            a_kv(0, 0)
            a_kv(0, 1)
            pe.wait_ge(S["pool_const"], NCONST)
            keep_warm(12)
            a_km(0)
            keep_warm(6)
            a_att(0, False)
            keep_warm(24)
            pe.wait_ge(S["w_lo"], W_OUT + 1)
            pe.wait_ge(S["bias_rows"], 3 * 16)
            a_out(0, True)
            keep_warm(21)
            turn_half("a1", X, xn_a, 0, 0, A1_FIRST)
            turn_half("a1", Y, xn_a, 0, 1, A1_FIRST)
            keep_warm(5)
            pe.wait_ge(S["w_lo"], NWT)
            pe.wait_ge(S["a1_xT_lo"], 1)
            phase_1(0, True, False, 0)
            phase_2(0, True, False, 0)
            pe.wait_ge(S["a1_xT_lo"], 2)
            with pe.Fori(1, NB - 1) as loop_i:
                i, run = turns(pe, loop_i)
                phase_1(i, True, True, run)
                phase_2(i, True, True, run + 1)
            phase_1(NB - 1, False, True, 2 * NB - 3)
            phase_2(NB - 1, False, True, 2 * NB - 2)
            b_out(NB - 1, True)
            keep_warm(18)
            turn_half("b3", X, xn_b, NB - 1, 0, B3_LAST)
            turn_half("b3", Y, xn_b, NB - 1, 1, B3_LAST)
            pe.wait_ge(S["b3_xT_lo"], NB)
            r = 2 * NB - 1
            f_router(r, x3T_s)
            f_h(r, 0, x3T_s)
            f_router_turn(r)
            f_h(r, 1, x3T_s)
            for f in range(NF):
                if f + 2 < NF:
                    f_h(r, f + 2, x3T_s)
                f_o(r, f, f == NF - 1)

        def q_exp(b):
            return tmp[:] if b == 0 else x2[:].rearrange("p (c t) d -> p c (t d)", c=C)

        def by_chunk(tiles):
            return tiles.rearrange("p t (c d) -> p t c d", c=C)

        @block.scalar
        def _(act):
            def take_hi(dst, src, ready, value, done):
                act.wait_ge(ready, value)
                act.activation(dst, src, ACT.Copy).then_inc(done, 1)

            def take_hi_half(dst, src, pre, b, half, place):
                tok = slice(half * (N // 2), (half + 1) * (N // 2))
                ready, value = norm_step(pre, "xnT", b, half, place)
                take_hi(dst[:, :, tok], src[:, :, tok], ready, value, norm_step(pre, "xT_hi", b, half, place)[0])

            def elu_parts(exp_dst, relu_dst, src, exp_done, relu_done):
                act.activation(exp_dst, src, ACT.Exp).then_inc(exp_done, 1)
                act.activation(relu_dst, src, ACT.Relu).then_inc(relu_done, 1)

            def a_q(b):
                act.wait_ge(S["a_q"], at(b, 1, 1))
                elu_parts(q_exp(b), q_f[:], Y[:], S["a_q_exp"], S["a_q_relu"])

            def a_kv(b, pair):
                src = (X, Y)[pair]
                act.wait_ge(S["a_kv"], at(b, 2, pair + 1))
                if b == 0 and pair == 0:
                    act.wait_ge(S["a_q_f"], 1)
                half = tmp[:, pair, :].rearrange("p (t d) -> p t d", t=2)
                tiles = slice(2 * pair, 2 * pair + 2)
                elu_parts(half, k_f[:, tiles, :], src[:, :, 0:D], S["a_kv_exp"], S["a_kv_relu"])
                act.activation(v_s[0][:, tiles, :, 0:P], by_chunk(src[:, :, D:2 * D]), ACT.Copy).then_inc(S["a_v_hi"], 1)

            def a_q_hi(b):
                act.wait_ge(S["a_q_f"], at(b, 1, 1))
                act.activation(qT_s[0][:], q_f[:], ACT.Copy).then_inc(S["a_q_hi"], 1)

            def a_den(b):
                if b == 0:
                    act.wait_ge(S["z_eps"], 1)
                for c in range(C):
                    act.wait_ge(S["a_den"], at(b, C, c + 1))
                    act.activation(tmp[:, c, :], Y[:, c, :], ACT.Identity, bias=z_eps[:, 0:1]) \
                        .then_inc(S["a_den_eps"], 1)

            def a_attn_hi(b, c):
                act.wait_ge(S["a_attn"], at(b, C, c + 1))
                act.activation(xT_s[0][:, c, :], q_f[:, c, :], ACT.Copy).then_inc(S["a_attn_hi"], 1)

            def f_logits_T(r):
                act.wait_ge(S["f_router"], at(r, 1, 1))
                act.activation(logits_T, O[:, 0, :], ACT.Copy).then_inc(S["f_logits_T"], 1)

            def f_gelu(r, f):
                act.wait_ge(S["f_h"], at(r, NF, f + 1))
                if not (r == 0 and f < 2):
                    act.wait_ge(S["f_h_lo"], at(r, NF, f - 1))
                if not (r == 0 and f < HR):
                    act.wait_ge(S["f_o"], at(r, NF, f + 1 - HR))
                act.activation(h_s[f % HR][0][:], H[f % 2][:], ACT.Gelu_apprx_tanh, bias=b1_sb[:, f:f + 1]) \
                    .then_inc(S["f_h_hi"], 1)
                act.activation(h_f[f % 2][:], H[f % 2][:], ACT.Gelu_apprx_tanh, bias=b1_sb[:, f:f + 1]) \
                    .then_inc(S["f_gelu"], 1)

            def f_exp(r):
                act.wait_ge(S["f_shift"], at(r, 1, 1))
                act.activation(top_p[:], top_p[:], ACT.Exp).then_inc(S["f_exp"], 1)

            def b_kq_gain(b, which, c, dst, done):
                g = 2 * C * which + c
                act.wait_ge(S[("b_kT", "b_qT")[which]], at(b, 1, 1))
                act.activation(dst, (Y, X)[which][:, c, :], ACT.Identity, bias=kq_gain_sb[:, g + C:g + C + 1],
                               scale=kq_gain_sb[:, g:g + 1]).then_inc(S[done], 1)

            def b_kq(b):
                for which in range(2):
                    for c in range(C):
                        if c == 1:
                            act.wait_ge(S[("b_kT_f", "b_qT_f1")[which]], at(b, (2, 1)[which], 1))
                        b_kq_gain(b, which, c, kqT_s[0][:, C * which + c, :], f"b_{'kq'[which]}T_hi")
                b_kq_gain(b, 1, 0, q_f[:, 0, :], "b_qT_f0")

            def b_v_hi(b):
                act.wait_ge(S["b_v_f"], at(b, 1, 1))
                act.activation(v_s[0][:, :, :, 0:P], by_chunk(v_f[:]), ACT.Copy).then_inc(S["b_v_hi"], 1)

            def b_exp(b, t):
                src = (Y, X)[t // 2]
                act.wait_ge(S["b_max"], at(b, 2, t // 2 + 1))
                act.activation(kq_n[:, t, :], src[:, t % 2, :], ACT.Exp, bias=row_negmax[:, t:t + 1],
                               accum_out=row_sum[:, t:t + 1]).then_inc(S["b_prob"], 1)

            def phase_1(i, has_a, has_prev, r):
                f_gelu(r, 0)
                f_gelu(r, 1)
                f_logits_T(r)
                f_gelu(r, 2)
                if has_a:
                    take_hi(xT_s[0][:], X[:], S["a_xnT"], at(i + 1, 1, 1), S["a_xT_hi"])
                f_gelu(r, 3)
                if has_a:
                    a_q(i + 1)
                    a_kv(i + 1, 0)
                    a_kv(i + 1, 1)
                    a_q_hi(i + 1)
                f_exp(r)
                if has_prev:
                    take_hi(x3T_s[0][:], X[:], S["b3_xnT"], at(i, 1, 0), S["b3_xT_hi"])
                f_gelu(r, 4)
                f_gelu(r, 5)
                if has_a:
                    a_den(i + 1)
                f_gelu(r, 6)
                if has_a:
                    a_attn_hi(i + 1, 0)
                f_gelu(r, 7)
                if has_a:
                    a_attn_hi(i + 1, 1)

            def phase_2(i, has_a, has_prev, r):
                if has_prev:
                    f_gelu(r, 0)
                    f_gelu(r, 1)
                    f_logits_T(r)
                    f_gelu(r, 2)
                if i == 0:
                    take_hi_half(b_in(i)[0], Y, "b", i, 0, B_FIRST)
                    take_hi_half(b_in(i)[0], O, "b", i, 1, B_FIRST)
                else:
                    take_hi(xT_s[0][:], Y[:], S["b_xnT"], at(i, 1, 1), S["b_xT_hi"])
                if has_prev:
                    f_gelu(r, 3)
                    f_gelu(r, 4)
                if has_a and i != 0:
                    take_hi(x1T_s[0][:], X[:], S["a1_xnT"], at(i, 1, 2), S["a1_xT_hi"])
                if has_prev:
                    f_exp(r)
                    f_gelu(r, 5)
                    f_gelu(r, 6)
                b_kq(i)
                if has_prev:
                    f_gelu(r, 7)
                b_v_hi(i)
                for t in range(T):
                    b_exp(i, t)
                if i == 0:
                    take_hi(x1T_s[0][:], O[:], S["a1_xnT"], 2, S["a1_xT_hi"])
                for pair in range(2):
                    take_hi(kqT_s[0][:, 2 * pair:2 * pair + 2, :], (Y, X)[pair][:], S["b_pT"], at(i, 2, pair + 1),
                            S["b_pT_hi"])

            def w_hi(n):
                src, dst, view = places[n]
                act.wait_ge(w_in[n], 16)
                if n == W_R:
                    act.wait_ge(S["pool_const"], NCONST)
                act.activation(dst[0][:, :, :], view, ACT.Copy).then_inc(S["w_hi"], 1)

            w_hi(W_QKV)
            w_hi(W_OUT)
            take_hi(xT_s[0][:], X[:], S["a_xnT"], 1, S["a_xT_hi"])
            w_hi(W_R)
            w_hi(W_1)
            a_q(0)
            act.wait_ge(S["w_lo"], W_OUT + 1)
            a_kv(0, 0)
            a_kv(0, 1)
            a_q_hi(0)
            w_hi(W_KQV)
            w_hi(W_2)
            a_den(0)
            a_attn_hi(0, 0)
            a_attn_hi(0, 1)
            act.wait_ge(S["w_lo"], W_KQV + 1)
            take_hi_half(x1T_s[0], X, "a1", 0, 0, A1_FIRST)
            take_hi_half(x1T_s[0], Y, "a1", 0, 1, A1_FIRST)
            act.wait_ge(S["small_in"], 5 * 16)
            phase_1(0, True, False, 0)
            phase_2(0, True, False, 0)
            with act.Fori(1, NB - 1) as loop_i:
                i, run = turns(act, loop_i)
                phase_1(i, True, True, run)
                phase_2(i, True, True, run + 1)
            phase_1(NB - 1, False, True, 2 * NB - 3)
            phase_2(NB - 1, False, True, 2 * NB - 2)
            take_hi_half(x3T_s[0], X, "b3", NB - 1, 0, B3_LAST)
            take_hi_half(x3T_s[0], Y, "b3", NB - 1, 1, B3_LAST)
            f_logits_T(2 * NB - 1)
            for f in range(NF):
                f_gelu(2 * NB - 1, f)
                if f == 1:
                    f_exp(2 * NB - 1)

        @block.vector
        def _(dve):

            dve_places = iter(range(SPARE))

            def carry():
                n = next(dve_places)
                dve.memset(spare_dve[:, n:n + 1], 0.0)

            def take_lo(dst, src, hi, ready, value, done):
                dve.wait_ge(ready, value)
                dve.tensor_tensor(dst, src, hi.bitcast(F32), ALU.subtract).then_inc(done, 1)

            def norm_stats(b, pre, src, st, mv, half=None, place=None):
                done, value = norm_step(pre, "stats", b, half, place)
                for t in tiles_of(half):
                    op = dve.bn_stats(st[:, t, :], src[:, t, :])
                op.then_inc(done, 1)
                dve.wait_ge(done, value)
                carry()
                for t in tiles_of(half):
                    op = dve.bn_aggr(mv[:, t, :], st[:, t, :])
                op.then_inc(norm_step(pre, "mv", b, half, place)[0], 1)

            def norm_apply(b, pre, src, dst, mv, rs, half=None, place=None):
                dve.wait_ge(*norm_step(pre, "rstd", b, half, place))
                for t in tiles_of(half):
                    op = dve.tensor_scalar(dst[:, t, :], src[:, t, :], mv[:, t, 0:1], rs[:, t:t + 1],
                                           ALU.subtract, ALU.mult)
                op.then_inc(norm_step(pre, "xn", b, half, place)[0], 1)

            def xT_lo_half(dst, src, hi, pre, b, half, place):
                tok = slice(half * (N // 2), (half + 1) * (N // 2))
                ready, value = norm_step(pre, "xT_hi", b, half, place)
                take_lo(dst[:, :, tok], src[:, :, tok], hi[:, :, tok], ready, value,
                        norm_step(pre, "xT_lo", b, half, place)[0])

            def a_stats(b):
                dve.wait_ge(S["x_in"], at(b, 16, 16))
                norm_stats(b, "a", x_in, stA, mvA)

            def a_norm(b):
                if b != 0:
                    dve.wait_ge(S["a1_xnT"], at(b, 1, 0))
                norm_apply(b, "a", x_in, xn_a, mvA, rsA)

            def elu(dst, exp, exp_done, relu_done, value, done):
                dve.wait_ge(relu_done, value)
                dve.wait_ge(exp_done, value)
                dve.scalar_tensor_tensor(dst, exp, 1.0, dst, ALU.min, ALU.add).then_inc(done, 1)

            def a_q(b):
                elu(q_f[:], q_exp(b), S["a_q_exp"], S["a_q_relu"], at(b, 1, 1), S["a_q_f"])

            def split_f(dst, src, pre, value):
                dve.wait_ge(S[f"{pre[0]}"], value)
                dve.tensor_copy(dst[0], src).then_inc(S[f"{pre[1]}_hi"], 1)
                take_lo(dst[1], src, dst[0], S[f"{pre[1]}_hi"], value, S[f"{pre[1]}_lo"])

            def a_q_lo(b):
                take_lo(qT_s[1][:], q_f[:], qT_s[0][:], S["a_q_hi"], at(b, 1, 1), S["a_q_lo"])

            def a_k(b, pair):
                tiles = slice(2 * pair, 2 * pair + 2)
                half = tmp[:, pair, :].rearrange("p (t d) -> p t d", t=2)
                elu(k_f[:, tiles, :], half, S["a_kv_exp"], S["a_kv_relu"], at(b, 2, pair + 1), S["a_k_f"])
                split_f([k[:, tiles, :] for k in k_s], k_f[:, tiles, :], ("a_k_f", "a_k"), at(b, 2, pair + 1))

            def a_v(b, pair):
                tiles = slice(2 * pair, 2 * pair + 2)
                take_lo(v_s[1][:, tiles, :, 0:P], by_chunk((X, Y)[pair][:, :, D:2 * D]), v_s[0][:, tiles, :, 0:P],
                        S["a_v_hi"], at(b, 2, pair + 1), S["a_v_lo"])

            def a_km(b):
                dve.wait_ge(S["a_q_lo"], at(b, 1, 1))
                dve.wait_ge(S["a_km"], at(b, 1, 1))
                mask = head_mask[:].unsqueeze(1).to_broadcast([P, C, P])
                dve.tensor_tensor(km_f[:, 0:C, :], Y[:, :, 0:P], mask, ALU.mult)
                dve.tensor_tensor(km_lo_f, Y[:, :, VW:VW + P], mask, ALU.mult).then_inc(S["a_km_part"], 1)
                dve.tensor_tensor(km_f[:, C:2 * C, :], Y[:, :, P:P + 1].to_broadcast([P, C, P]), mask, ALU.mult)
                dve.wait_ge(S["a_km_part"], at(b, 1, 1))
                dve.tensor_tensor(km_f[:, 0:C, :], km_f[:, 0:C, :], km_lo_f, ALU.add).then_inc(S["a_km_f"], 1)
                split_f([km[:] for km in km_s], km_f, ("a_km_f", "a_km"), at(b, 1, 1))

            def a_z(b, c, half):
                if half == 0:
                    dve.wait_ge(S["a_den_eps"], at(b, C, c + 1))
                tok = slice(half * (N // 2), (half + 1) * (N // 2))
                dve.reciprocal(tmp[:, c, tok], tmp[:, c, tok]).then_inc(S["a_z"], 1)

            def a_attn(b, c):
                dve.wait_ge(S["a_z"], at(b, 2 * C, 2 * c + 2))
                dve.wait_ge(S["a_att"], at(b, C, C))
                if c == 0:
                    dve.wait_ge(S["a_km_lo"], at(b, 1, 1))
                dve.tensor_tensor(q_f[:, c, :], X[:, c, :], tmp[:, c, :], ALU.mult).then_inc(S["a_attn"], 1)

            def a_attn_lo(b, c):
                take_lo(xT_s[1][:, c, :], q_f[:, c, :], xT_s[0][:, c, :], S["a_attn_hi"], at(b, C, c + 1), S["a_attn_lo"])

            def a_x1(b, half=None):
                dve.wait_ge(*step("a_out", "out", b, half, A1_FIRST))
                dve.wait_ge(S["a_res"], at(b, 1, 1))
                if b != 0:
                    dve.wait_ge(S["f_y"], at(b, 2, -2) if b != 1 else 1)
                banks = slice(0, 2) if half is None else slice(half, half + 1)
                dve.tensor_tensor(x1[:].rearrange("p (a t) d -> p a (t d)", a=2)[:, banks, :], X[:, banks, :],
                                  x_in[:].rearrange("p (a t) d -> p a (t d)", a=2)[:, banks, :], ALU.add) \
                    .then_inc(step("a_x1", "sum", b, half, A1_FIRST)[0], 1)

            def a1_stats(b, half=None):
                dve.wait_ge(*step("a_x1", "sum", b, half, A1_FIRST))
                norm_stats(b, "a1", x1, stA, mvA, half, A1_FIRST)

            def a1_norm(b):
                norm_apply(b, "a1", x1, xn_a, mvA, rsA)

            def f_logits(r):
                rows = O[:, 1, :].rearrange("p (t n) -> p t n", t=T)
                dve.wait_ge(S["f_router_turn"], at(r, 1, 1))
                dve.tensor_copy(logit_hi[:], rows[:, :, 0:E]).then_inc(S["f_logit_hi"], 1)
                dve.wait_ge(S["f_logit_hi"], at(r, 1, 1))
                dve.tensor_tensor(logits[:], rows[:, :, E:2 * E], logit_hi[:], ALU.add).then_inc(S["f_logits"], 1)

            def f_top(r):
                dve.wait_ge(S["f_logits"], at(r, 1, 1))
                carry()
                for t in range(T):
                    op = dve.max(top[:, t, :], logits[:, t, :])
                op.then_inc(S["f_top"], 1)
                dve.wait_ge(S["f_top"], at(r, 1, 1))
                dve.tensor_tensor(top_p[:], top[:], top[:, :, 0:1].to_broadcast([P, T, E]), ALU.subtract) \
                    .then_inc(S["f_shift"], 1)

            def f_comb(r):
                dve.wait_ge(S["f_exp"], at(r, 1, 1))
                dve.tensor_reduce(p_sum[:], top_p[:], X_AXIS, ALU.add).then_inc(S["f_psum"], 1)
                dve.wait_ge(S["f_psum"], at(r, 1, 1))
                dve.reciprocal(p_rec[:], p_sum[:]).then_inc(S["f_prec"], 1)
                dve.wait_ge(S["f_prec"], at(r, 1, 1))
                dve.tensor_tensor(p2[:], top_p[:, :, 0:2], p_rec[:].unsqueeze(2).to_broadcast([P, T, 2]), ALU.mult) \
                    .then_inc(S["f_p2"], 1)
                dve.wait_ge(S["f_p2"], at(r, 1, 1))
                dve.tensor_tensor(t_sum[:], p2[:, :, 0], p2[:, :, 1], ALU.add).then_inc(S["f_tsum"], 1)
                dve.wait_ge(S["f_tsum"], at(r, 1, 1))
                dve.reciprocal(t_rec[:], t_sum[:]).then_inc(S["f_trec"], 1)
                dve.wait_ge(S["f_trec"], at(r, 1, 1))
                dve.tensor_tensor(p2[:], p2[:], t_rec[:].unsqueeze(2).to_broadcast([P, T, 2]), ALU.mult) \
                    .then_inc(S["f_comb_p"], 1)
                dve.wait_ge(S["f_comb_p"], at(r, 1, 1))
                dve.tensor_tensor(comb[:], p2[:, :, 0], p2[:, :, 1], ALU.add).then_inc(S["f_comb"], 1)

            def f_lo(r, f):
                if not (r == 0 and f < HR):
                    dve.wait_ge(S["f_o"], at(r, NF, f + 1 - HR))
                take_lo(h_s[f % HR][1][:], h_f[f % 2][:], h_s[f % HR][0][:], S["f_gelu"], at(r, NF, f + 1), S["f_h_lo"])

            def f_y_tile(t, res, dst):
                return dve.scalar_tensor_tensor(dst[:, t, :], O[:, t // 2, (t % 2) * D:(t % 2 + 1) * D],
                                                comb[:, t:t + 1], res[:, t, :], ALU.mult, ALU.add)

            def f_y(r, res, dst, b=None, half=None):
                dve.wait_ge(S["f_comb"], at(r, 1, 1))
                dve.wait_ge(S["f_res"], at(r, 1, 1))
                if half == 0:
                    dve.wait_ge(S["half_out"], B_FIRST + 1)
                else:
                    dve.wait_ge(S["f_o"], at(r, NF, NF))
                if b is not None:
                    dve.wait_ge(S["b_res"], at(b, 1, 1))
                for t in tiles_of(half):
                    op = f_y_tile(t, res, dst)
                op.then_inc(step("f_y", "sum", r, half, B_FIRST)[0], 1)

            def b_norm(b, has_prev, half=None):
                if has_prev:
                    dve.wait_ge(S["f_y"], at(b, 2, 0))
                    dve.wait_ge(S["b3_xnT"], at(b, 1, 0))
                else:
                    dve.wait_ge(*step("f_y", "sum", 0, half, B_FIRST))
                norm_stats(b, "b", x2, stF, mvF, half, B_FIRST)

            def b_kqv(b, t):
                src = (Y, X)[t % 2]
                parts = (src[:, 0, 0:D], src[:, 0, D:2 * D], src[:, 1, 0:D])
                dve.wait_ge(S["b_kqv"], at(b, T, t + 1))
                for n in range(3):
                    op = dve.bn_stats(stK[:, t, n, :], parts[n])
                op.then_inc(S["b_kqv_stats"], 1)
                dve.wait_ge(S["b_kqv_stats"], at(b, T, t + 1))
                carry()
                for n in range(3):
                    op = dve.bn_aggr(mvK[:, t, n, :], stK[:, t, n, :])
                op.then_inc(S["b_kqv_mv"], 1)

            def b_kqv_n(b, t):
                src = (Y, X)[t % 2]
                dsts = (kq_n[:, t, 0:D], kq_n[:, t, D:2 * D], v_f[:, t, :])
                parts = (src[:, 0, 0:D], src[:, 0, D:2 * D], src[:, 1, 0:D])
                dve.wait_ge(S["b_kqv_rstd"], at(b, T, t + 1))
                for n in range(3):
                    op = dve.tensor_scalar(dsts[n], parts[n], mvK[:, t, n, 0:1], rsK[:, t, n:n + 1],
                                           ALU.subtract, ALU.mult)
                    if n == 1:
                        op.then_inc(S["b_kq_n"], 1)
                op.then_inc(S["b_kqv_n"], 1)

            def b_gain(dst, src, which, c):
                g = 2 * C * which + c
                return dve.tensor_scalar(dst[:, c, :], src[:, c, :], kq_gain_sb[:, g:g + 1],
                                         kq_gain_sb[:, g + C:g + C + 1], ALU.mult, ALU.add)

            def b_kq(b):
                dve.wait_ge(S["b_kT"], at(b, 1, 1))
                b_gain(tmp, Y, 0, 1).then_inc(S["b_kT_f"], 1)
                dve.wait_ge(S["b_kT_hi"], at(b, C, 1))
                b_gain(tmp, Y, 0, 0).then_inc(S["b_kT_f"], 1)
                dve.wait_ge(S["b_qT"], at(b, 1, 1))
                b_gain(q_f, X, 1, 1).then_inc(S["b_qT_f1"], 1)
                dve.wait_ge(S["b_kT_hi"], at(b, C, C))
                take_lo(kqT_s[1][:, 0:C, :], tmp[:], kqT_s[0][:, 0:C, :], S["b_kT_f"], at(b, C, C), S["b_kT_lo"])
                dve.wait_ge(S["b_qT_hi"], at(b, C, C))
                for c, full in ((1, "b_qT_f1"), (0, "b_qT_f0")):
                    take_lo(kqT_s[1][:, C + c, :], q_f[:, c, :], kqT_s[0][:, C + c, :], S[full], at(b, 1, 1), S["b_qT_lo"])

            def b_v_lo(b):
                take_lo(v_s[1][:, :, :, 0:P], by_chunk(v_f[:]), v_s[0][:, :, :, 0:P], S["b_v_hi"], at(b, 1, 1),
                        S["b_v_lo"])

            def b_max(b, pair):
                dve.wait_ge(S["b_sc"], at(b, 2, pair + 1))
                dve.tensor_reduce(row_negmax[:, 2 * pair:2 * pair + 2], (Y, X)[pair][:], X_AXIS, ALU.max,
                                  negate=True).then_inc(S["b_max"], 1)

            def b_pT_lo(b, pair):
                js = slice(2 * pair, 2 * pair + 2)
                take_lo(kqT_s[1][:, js, :], (Y, X)[pair][:], kqT_s[0][:, js, :], S["b_pT_hi"], at(b, 2, pair + 1),
                        S["b_pT_lo"])

            def b_x3(b, half=None):
                if half != 1:
                    dve.wait_ge(S["b_prob"], at(b, T, T))
                    dve.reciprocal(row_rec[:], row_sum[:]).then_inc(S["b_rec"], 1)
                    dve.wait_ge(S["b_rec"], at(b, 1, 1))
                    dve.wait_ge(S["b_res"], at(b, 1, 1))
                dve.wait_ge(*step("b_out", "out", b, half, B3_LAST))
                for t in tiles_of(half):
                    op = dve.scalar_tensor_tensor(x3[:, t, :], Y[:, t // 2, (t % 2) * D:(t % 2 + 1) * D],
                                                  row_rec[:, t:t + 1], x2[:, t, :], ALU.mult, ALU.add)
                op.then_inc(step("b_x3", "sum", b, half, B3_LAST)[0], 1)

            def b3_stats(b, half=None):
                dve.wait_ge(*step("b_x3", "sum", b, half, B3_LAST))
                norm_stats(b, "b3", x3, stF, mvF, half, B3_LAST)

            def b3_norm(b, half=None):
                if not (b == 0):
                    dve.wait_ge(S["x_out"], at(b, 16, 16))
                norm_apply(b, "b3", x3, xn_b, mvF, rsF, half, B3_LAST)

            def xT_lo(dst, src, hi, pre, b):
                take_lo(dst[:], src[:], hi[:], S[f"{pre}_xT_hi"], at(b, 1, 1), S[f"{pre}_xT_lo"])

            def phase_1(i, has_a, has_prev, r):
                if has_a:
                    a_stats(i + 1)
                if i == 0:
                    a_norm(i + 1)
                f_lo(r, 0)
                f_lo(r, 1)
                if has_a and i != 0:
                    a_norm(i + 1)
                if has_prev:
                    b_x3(i - 1)
                    b3_stats(i - 1)
                if has_a:
                    xT_lo(xT_s[1], X, xT_s[0], "a", i + 1)
                f_lo(r, 2)
                f_logits(r)
                f_top(r)
                if has_prev:
                    b3_norm(i - 1)
                if has_a:
                    a_q(i + 1)
                f_lo(r, 3)
                if has_a:
                    a_v(i + 1, 0)
                    a_k(i + 1, 0)
                    a_v(i + 1, 1)
                    a_k(i + 1, 1)
                    a_q_lo(i + 1)
                f_comb(r)
                if has_prev:
                    xT_lo(x3T_s[1], X, x3T_s[0], "b3", i - 1)
                f_lo(r, 4)
                if has_a:
                    a_km(i + 1)
                f_lo(r, 5)
                if has_a:
                    a_z(i + 1, 0, 0)
                    a_z(i + 1, 0, 1)
                f_lo(r, 6)
                if has_a:
                    a_attn(i + 1, 0)
                    a_z(i + 1, 1, 0)
                f_lo(r, 7)
                if has_a:
                    a_z(i + 1, 1, 1)
                if i == 0:
                    for half in range(2):
                        f_y(r, x1, x2, half=half)
                        b_norm(i, has_prev, half)
                    norm_apply(i, "b", x2, xn_b, mvF, rsF, 0, B_FIRST)
                    a_attn(i + 1, 1)
                    norm_apply(i, "b", x2, xn_b, mvF, rsF, 1, B_FIRST)
                elif has_a:
                    a_attn(i + 1, 1)
                if i != 0:
                    f_y(r, x1, x2)
                if has_a:
                    a_attn_lo(i + 1, 0)
                    a_attn_lo(i + 1, 1)
                if i != 0:
                    b_norm(i, has_prev)

            def phase_2(i, has_a, has_prev, r):
                if i == 0:
                    for half in range(2):
                        xT_lo_half(b_in(i)[1], (Y, O)[half], b_in(i)[0], "b", i, half, B_FIRST)
                    a_x1(i + 1)
                else:
                    f_lo(r, 0)
                    if has_a:
                        a_x1(i + 1)
                    norm_apply(i, "b", x2, xn_b, mvF, rsF)
                    f_logits(r)
                    if has_a:
                        a1_stats(i + 1)
                    f_lo(r, 1)
                    f_lo(r, 2)
                    if has_a:
                        a1_norm(i + 1)
                    xT_lo(xT_s[1], Y, xT_s[0], "b", i)
                    f_top(r)
                    f_lo(r, 3)
                    if has_a:
                        xT_lo(x1T_s[1], X, x1T_s[0], "a1", i + 1)
                b_kqv(i, 0)
                if has_prev:
                    f_lo(r, 4)
                b_kqv(i, 1)
                b_kqv_n(i, 0)
                b_kqv_n(i, 1)
                if has_prev:
                    f_lo(r, 5)
                else:
                    a1_stats(i + 1)
                b_kqv(i, 2)
                b_kqv(i, 3)
                b_kqv_n(i, 2)
                b_kqv_n(i, 3)
                b_kq(i)
                if i == 0:
                    a1_norm(i + 1)
                if has_prev:
                    f_lo(r, 6)
                    f_comb(r)
                    f_lo(r, 7)
                b_max(i, 0)
                b_max(i, 1)
                b_v_lo(i)
                if i == 0:
                    xT_lo(x1T_s[1], O, x1T_s[0], "a1", i + 1)
                b_pT_lo(i, 0)
                b_pT_lo(i, 1)
                if has_prev:
                    f_y(r, x3, xn_b, i)

            def w_lo(n):
                src, dst, view = places[n]
                take_lo(dst[1][:, :, :], view, dst[0][:, :, :], S["w_hi"], n + 1, S["w_lo"])

            dve.memset(z_eps[:], 1e-6).then_inc(S["z_eps"], 1)
            a_stats(0)
            a_norm(0)
            w_lo(W_QKV)
            w_lo(W_OUT)
            xT_lo(xT_s[1], X, xT_s[0], "a", 0)
            w_lo(W_R)
            w_lo(W_1)
            a_q(0)
            for pair in range(2):
                a_k(0, pair)
                a_v(0, pair)
            a_q_lo(0)
            a_km(0)
            w_lo(W_KQV)
            for c in range(C):
                a_z(0, c, 0)
                a_z(0, c, 1)
                a_attn(0, c)
            for c in range(C):
                a_attn_lo(0, c)
            w_lo(W_2)
            for half in range(2):
                a_x1(0, half)
                a1_stats(0, half)
            for half in range(2):
                norm_apply(0, "a1", x1, xn_a, mvA, rsA, half, A1_FIRST)
            for half in range(2):
                xT_lo_half(x1T_s[1], (X, Y)[half], x1T_s[0], "a1", 0, half, A1_FIRST)
            phase_1(0, True, False, 0)
            phase_2(0, True, False, 0)
            with dve.Fori(1, NB - 1) as loop_i:
                i, run = turns(dve, loop_i)
                phase_1(i, True, True, run)
                phase_2(i, True, True, run + 1)
            phase_1(NB - 1, False, True, 2 * NB - 3)
            phase_2(NB - 1, False, True, 2 * NB - 2)
            for half in range(2):
                b_x3(NB - 1, half)
                b3_stats(NB - 1, half)
            for half in range(2):
                b3_norm(NB - 1, half)
            for half in range(2):
                xT_lo_half(x3T_s[1], (X, Y)[half], x3T_s[0], "b3", NB - 1, half, B3_LAST)
            r = 2 * NB - 1
            f_logits(r)
            f_top(r)
            for f in range(NF):
                f_lo(r, f)
                if f == 3:
                    f_comb(r)
            dve.wait_ge(S["f_comb"], at(r, 1, 1))
            dve.wait_ge(S["f_res"], at(r, 1, 1))
            for t in range(T):
                if t % 2 == 0:
                    dve.wait_ge(*((S["half_out"], F_LAST + 1) if t == 0 else (S["f_o"], at(r, NF, NF))))
                f_y_tile(t, x3, xn_b).then_inc(S["f_y_tile"], 1)

        @block.gpsimd
        def _(pool):

            pool_places = iter(range(SPARE))

            def carry():
                n = next(pool_places)
                pool.tensor_tensor(spare_pool[:, n:n + 1], neg_half[:, 0:1], neg_half[:, 0:1], ALU.mult)

            def rstd(dst, ve, mv, ready, added, done, width):
                pool.wait_ge(*ready)
                carry()
                pool.tensor_scalar(ve, mv, EPS, None, ALU.add).then_inc(added[0], 1)
                pool.wait_ge(*added)
                pool.tensor_tensor(dst, ve, neg_half[:, 0:width], ALU.pow).then_inc(done, 1)

            def norm_rstd(b, pre, ve, mv, rs, half=None, place=None):
                tiles = slice(tiles_of(half)[0], tiles_of(half)[-1] + 1)
                rstd(rs[:, tiles], ve[:, tiles], mv[:, tiles, 1], norm_step(pre, "mv", b, half, place),
                     norm_step(pre, "ve", b, half, place), norm_step(pre, "rstd", b, half, place)[0], len(tiles_of(half)))

            def a_res(b):
                pool.wait_ge(S["a_xn"], at(b, 1, 1))
                pool.tensor_tensor(x_in[:], x_in[:], bout_sb[:].unsqueeze(1).to_broadcast([P, T, D]), ALU.add) \
                    .then_inc(S["a_res"], 1)

            def f_res(r, res):
                pool.wait_ge(S["f_comb"], at(r, 1, 1))
                pool.tensor_tensor(b2_comb[:], b2_sb[:].unsqueeze(1).to_broadcast([P, T, D]),
                                   comb[:].unsqueeze(2).to_broadcast([P, T, D]), ALU.mult).then_inc(S["f_b2"], 1)
                pool.wait_ge(S["f_b2"], at(r, 1, 1))
                pool.tensor_tensor(res[:], res[:], b2_comb[:], ALU.add).then_inc(S["f_res"], 1)

            def b_res(b):
                pool.wait_ge(S["b_xn"], at(b, 1, 1))
                pool.tensor_tensor(x2[:], x2[:], xn_b[:], ALU.add).then_inc(S["b_res"], 1)

            def b_kqv_rstd(b, t):
                count = at(b, T, t + 1)
                rstd(rsK[:, t, :], veK[:, t, :], mvK[:, t, :, 1], (S["b_kqv_mv"], count), (S["b_kqv_ve"], count),
                     S["b_kqv_rstd"], 3)

            def b_v(b):
                pool.wait_ge(S["b_kqv_n"], at(b, T, T))
                pool.tensor_tensor(v_f[:], v_f[:], v_gain_sb[:].unsqueeze(1).to_broadcast([P, T, D]), ALU.mult) \
                    .then_inc(S["b_v_g"], 1)
                pool.wait_ge(S["b_v_g"], at(b, 1, 1))
                pool.tensor_tensor(v_f[:], v_f[:], v_beta_sb[:].unsqueeze(1).to_broadcast([P, T, D]), ALU.add) \
                    .then_inc(S["b_v_f"], 1)

            def phase_1(i, has_a, has_prev, r):
                if has_a:
                    norm_rstd(i + 1, "a", veA, mvA, rsA)
                if has_prev:
                    norm_rstd(i - 1, "b3", veF, mvF, rsF)
                if has_a:
                    a_res(i + 1)
                f_res(r, x1)
                for half in (0, 1) if i == 0 else (None,):
                    norm_rstd(i, "b", veF, mvF, rsF, half, B_FIRST)

            def phase_2(i, has_a, has_prev, r):
                if i != 0:
                    if has_a:
                        norm_rstd(i + 1, "a1", veA, mvA, rsA)
                    b_res(i)
                for t in range(T):
                    b_kqv_rstd(i, t)
                    if i == 0 and t == 1:
                        norm_rstd(i + 1, "a1", veA, mvA, rsA)
                if i == 0:
                    b_res(i)
                b_v(i)
                if has_prev:
                    f_res(r, x3)

            done = 0

            def const(op):
                nonlocal done
                op.then_inc(S["pool_const"], 1)
                done += 1
                pool.wait_ge(S["pool_const"], done)

            const(pool.memset(neg_half[:], -0.5))
            const(pool.memset(ones_b[:], 1.0))
            const(pool.memset(ident[:], 0.0))
            const(pool.affine_select(out=ident[:], in_=ident[:], compare_op=ALU.not_equal, fill=1.0, base=0,
                                     pattern=[[-1, P]], channel_multiplier=1))
            norm_rstd(0, "a", veA, mvA, rsA)
            const(pool.memset(head_mask[:], 1.0))
            by_head = head_mask[:].rearrange("p (h d) -> p h d", d=HD)
            const(pool.affine_select(out=by_head, in_=by_head, compare_op=ALU.is_ge, fill=0.0, base=0,
                                     pattern=[[-HD, P // HD], [0, HD]], channel_multiplier=1))
            const(pool.affine_select(out=by_head, in_=by_head, compare_op=ALU.is_ge, fill=0.0, base=HD - 1,
                                     pattern=[[HD, P // HD], [0, HD]], channel_multiplier=-1))
            const(pool.memset(wr_s[:].bitcast(F32), 0.0))
            for part in range(2):
                const(pool.memset(v_s[part][:, :, :, P:VW].bitcast(F32), 1.0 - part))
            pool.memset(bkqv_rows[:], 0.0).then_inc(S["zeroed"], 1)
            pool.wait_ge(S["bias_in"], 16)
            pool.tensor_copy(bias_b[0:1, 0, :], bias_f[:]).then_inc(S["bias_part"], 1)
            for n in range(1, 3):
                pool.wait_ge(S["bias_part"], 2 * n - 1)
                pool.tensor_tensor(bias_f[:], bias_f[:], bias_b[0:1, n - 1, :], ALU.subtract) \
                    .then_inc(S["bias_part"], 1)
                pool.wait_ge(S["bias_part"], 2 * n)
                pool.tensor_copy(bias_b[0:1, n, :], bias_f[:]).then_inc(S["bias_part"], 1)
            pool.wait_ge(S["small_in"], 5 * 16)
            pool.wait_ge(S["x_out"], 16)
            a_res(0)
            for half in range(2):
                norm_rstd(0, "a1", veA, mvA, rsA, half, A1_FIRST)
            phase_1(0, True, False, 0)
            phase_2(0, True, False, 0)
            with pool.Fori(1, NB - 1) as loop_i:
                i, run = turns(pool, loop_i)
                phase_1(i, True, True, run)
                phase_2(i, True, True, run + 1)
            phase_1(NB - 1, False, True, 2 * NB - 3)
            phase_2(NB - 1, False, True, 2 * NB - 2)
            for half in range(2):
                norm_rstd(NB - 1, "b3", veF, mvF, rsF, half, B3_LAST)
            f_res(2 * NB - 1, x3)


def kernel(**inputs):
    import numpy as np
    import concourse.bacc as bacc
    from concourse.bass_utils import run_bass_kernel_spmd

    g = {name: np.asarray(a) for name, a in inputs.items()}

    def cols(v):
        return v.reshape(-1, P).T

    b = "L0_attn_b_"
    arrays = {
        "x": g["L0_attn_a_x"],
        "w_qkv": g["L0_attn_a_w_qkv"].T,
        "w_out": g["L0_attn_a_w_out"].T,
        "b_out": g["L0_attn_a_b_out"],
        "w_kqv": np.concatenate([g[b + "Wk"], g[b + "Wq"], g[b + "Wv"]], axis=1),
        "b_kqv": np.concatenate([g[b + "bk"], g[b + "bq"], g[b + "bv"]]).reshape(1, -1),
        "kq_gain": np.concatenate([cols(g[b + n]) for n in ("gk", "betak", "gq", "betaq")], axis=1),
        "v_gain": g[b + "gv"],
        "v_beta": g[b + "betav"],
        "router_w": g["L0_ffn_router_w"],
        "w1": g["L0_ffn_w1"],
        "b1": cols(g["L0_ffn_b1"]),
        "w2": g["L0_ffn_w2"],
        "b2": g["L0_ffn_b2"],
    }
    arrays = {name: np.ascontiguousarray(a) for name, a in arrays.items()}
    nc = bacc.Bacc("TRN2", target_bir_lowering=False, num_devices=1)
    args = [nc.dram_tensor(name, a.shape, mybir.dt.from_np(a.dtype), kind="ExternalInput").ap()
            for name, a in arrays.items()]
    out = nc.dram_tensor("out", arrays["x"].shape, F32, kind="ExternalOutput").ap()
    hybrid_block(nc, *args, out)
    r = run_bass_kernel_spmd(nc, [arrays], core_ids=[0])
    return r.results[0]["out"]
```
